# Optimizing a Trainium2 kernel written in Bass

```python
import numpy as np
import jax
import jax.numpy as jnp

def _softmax(x, axis=-1):
    return jax.nn.softmax(x, axis=axis)
def _gelu(x):
    return jax.nn.gelu(x, approximate=True)
def _silu(x):
    return jax.nn.silu(x)
def _sigmoid(x):
    return jax.nn.sigmoid(x)
def _layernorm(x, axis=-1, eps=1e-5):
    m = jnp.mean(x, axis=axis, keepdims=True)
    v = jnp.var(x, axis=axis, keepdims=True)
    return (x - m) / jnp.sqrt(v + eps)
def _scatter_add(tgt, idx, src, axis=0):
    return tgt.at[idx].add(src)
def _segment_sum(src, seg, n):
    return jax.ops.segment_sum(src, seg, n)

kernel_name = 'mk_adj_preln_d1_adj_256_e1df86'

def setup_inputs(seed: int = 0):
    np.random.seed(seed)
    _w = jnp.asarray
    def _rec_inputs():
        import jax
        import jax.numpy as jnp
        _gk = jax.random.key(seed)
        x = -0.0005207 + 1.001 * jax.random.normal(jax.random.fold_in(_gk, 1), (4096, 256), jnp.float32)
        _a = jax.random.bernoulli(jax.random.fold_in(_gk, 2), 0.00195312, (4096, 4096))
        _a = jnp.logical_or(_a, jnp.eye(4096, dtype=bool))
        _af = _a.astype(jnp.float32)
        _af = _af * jax.random.uniform(jax.random.fold_in(_gk, 3), (4096, 4096), jnp.float32, 0.05, 1)
        adj = _af
        return x, adj
    x, adj = _rec_inputs()
    def _L0_gnn_setup():
        import jax, jax.numpy as jnp
        import numpy as np
        D_IN = 256
        D_ATTN = 64
        STEPS = 2
        TOP_P = 0.9
        TAU = 1.0
        LN_EPS = 1e-05
        N_NODES = 8192

        def _top_p_attention(X, W1, W2, W3):
            q = X @ W1.T @ W2.T
            k = X @ W3.T
            logits = q @ k.T / TAU
            probs = jax.nn.softmax(logits, axis=-1)
            idx = jnp.argsort(-probs, axis=-1)
            sp = jnp.take_along_axis(probs, idx, axis=-1)
            cs = jnp.cumsum(sp, axis=-1)
            keep_sorted = cs - sp < TOP_P
            rows = jnp.arange(probs.shape[0])[:, None]
            mask = jnp.zeros(probs.shape, dtype=bool).at[rows, idx].set(keep_sorted)
            A = probs * mask
            return A / jnp.maximum(A.sum(-1, keepdims=True), 1e-12)
        key = jax.random.key(seed)
        ks = jax.random.split(key, 8)
        N, d, da, steps = (N_NODES, D_IN, D_ATTN, STEPS)
        X = jax.random.normal(ks[0], (N, d), dtype=jnp.float32)
        S = jax.random.uniform(ks[1], (N, N), dtype=jnp.float32)
        W1 = jax.random.normal(ks[2], (da, d), dtype=jnp.float32) / np.sqrt(d)
        W2 = jax.random.normal(ks[3], (da, da), dtype=jnp.float32) / np.sqrt(da)
        W3 = jax.random.normal(ks[4], (da, d), dtype=jnp.float32) / np.sqrt(d)
        U1 = jax.random.normal(ks[5], (steps, d, d), dtype=jnp.float32) / np.sqrt(d)
        U2 = jax.random.normal(ks[6], (steps, d, d), dtype=jnp.float32) / np.sqrt(d)
        ln_g = jnp.ones((d,), dtype=jnp.float32)
        ln_b = jnp.zeros((d,), dtype=jnp.float32)
        return {'X': X, 'S': S, 'W1': W1, 'W2': W2, 'W3': W3, 'U1': U1, 'U2': U2, 'ln_g': ln_g, 'ln_b': ln_b}
    _L0_gnn_all = _L0_gnn_setup()
    _L0_gnn_in = {k: v for k, v in _L0_gnn_all.items() if k in ('W1', 'W2', 'W3', 'U1', 'U2', 'ln_g', 'ln_b', )}
    del _L0_gnn_all

    return {
        "x": x,
        "adj": adj,
        "L0_gnn_W1": _L0_gnn_in["W1"],
        "L0_gnn_W2": _L0_gnn_in["W2"],
        "L0_gnn_W3": _L0_gnn_in["W3"],
        "L0_gnn_U1": _L0_gnn_in["U1"],
        "L0_gnn_U2": _L0_gnn_in["U2"],
        "L0_gnn_ln_g": _L0_gnn_in["ln_g"],
        "L0_gnn_ln_b": _L0_gnn_in["ln_b"],
    }

def reference(x, adj, L0_gnn_W1, L0_gnn_W2, L0_gnn_W3, L0_gnn_U1, L0_gnn_U2, L0_gnn_ln_g, L0_gnn_ln_b):
    import jax
    import jax.numpy as jnp
    def _L0_gnn_ref(X, S, W1, W2, W3, U1, U2, ln_g, ln_b):
        import jax, jax.numpy as jnp
        import numpy as np
        D_IN = 256
        D_ATTN = 64
        STEPS = 2
        TOP_P = 0.9
        TAU = 1.0
        LN_EPS = 1e-05
        N_NODES = 8192

        def _top_p_attention(X, W1, W2, W3):
            q = X @ W1.T @ W2.T
            k = X @ W3.T
            logits = q @ k.T / TAU
            probs = jax.nn.softmax(logits, axis=-1)
            idx = jnp.argsort(-probs, axis=-1)
            sp = jnp.take_along_axis(probs, idx, axis=-1)
            cs = jnp.cumsum(sp, axis=-1)
            keep_sorted = cs - sp < TOP_P
            rows = jnp.arange(probs.shape[0])[:, None]
            mask = jnp.zeros(probs.shape, dtype=bool).at[rows, idx].set(keep_sorted)
            A = probs * mask
            return A / jnp.maximum(A.sum(-1, keepdims=True), 1e-12)
        N = X.shape[0]
        R = S + jnp.eye(N, dtype=X.dtype)
        R = R / R.sum(-1, keepdims=True)
        Z = jnp.zeros_like(X)
        Xf = X
        Xa = X
        for n in range(STEPS):
            A = _top_p_attention(Xa, W1, W2, W3)
            Xf = R @ Xf
            Xa = A @ Xa
            Z = Z + Xf @ U1[n].T + Xa @ U2[n].T
        h = X + Z
        mu = h.mean(-1, keepdims=True)
        var = jnp.mean((h - mu) ** 2, axis=-1, keepdims=True)
        return (h - mu) / jnp.sqrt(var + LN_EPS) * ln_g + ln_b

    h = jnp.maximum(_layernorm(x, axis=-1), 0.0)
    x = x + _L0_gnn_ref(h, adj, L0_gnn_W1, L0_gnn_W2, L0_gnn_W3, L0_gnn_U1, L0_gnn_U2, L0_gnn_ln_g, L0_gnn_ln_b)
    return x


_drawn_inputs = setup_inputs


def setup_inputs(seed=0):
    import zlib

    import numpy as np

    out = dict(_drawn_inputs(seed))
    spreads = {'L0_gnn_ln_g': (1.0, 0.2), 'L0_gnn_ln_b': (0.0, 0.1)}
    factors = {}
    for name, (base, spread) in spreads.items():
        noise = np.random.default_rng([zlib.crc32(name.encode()), seed]).standard_normal(out[name].shape)
        drawn = base * np.exp(spread * noise) if base else spread * noise
        out[name] = jnp.asarray(drawn.astype(out[name].dtype))
    for name, factor in factors.items():
        out[name] = (out[name] * factor).astype(out[name].dtype)
    return out
```

```python
from contextlib import ExitStack
import math

import concourse.bass as bass
from concourse import mybir
from concourse.alu_op_type import AluOpType as ALU

ACT = mybir.ActivationFunctionType
AX = mybir.AxisListType.X
F32 = mybir.dt.float32
F32R = mybir.dt.float32r
I32 = mybir.dt.int32
U8 = mybir.dt.uint8

P = 128
TOP_P = 0.9
LN_EPS = 1e-5

EVALS = 3
SEGS = 16
CANDS = 8 * SEGS
ROUNDS = 5
DEPTH = 8 * ROUNDS
MARGIN = 16.0
FEW = 36.0
RELAX = 0.82
QP = 0.135
QS = 0.1975
DENSITY = 0.1755
REFINES = 8
GUESS = [(0.00537, 3.47), (0.526, 4096.0)]


def quantile_of(p):
    def power(x):
        e = math.floor(math.log2(x))
        return 2.0 ** (QP * (e + x / 2.0 ** e - 1.0))
    return (power(p) - power(1 - p)) / QS


def adj_preln_kernel(nc, x_d, adj_d, w1_d, w2t_d, w3t_d, u1t_d, u2t_d, g_d, b_d, out_d):
    NT, _, D = x_d.shape
    N = NT * P
    STEPS = u1t_d.shape[0]
    A = w1_d.shape[0]
    KT = D // P
    LC = 1024
    NLC = N // LC
    NPC = 8
    PJ = NT // NPC
    RING = 4
    W = D + 1
    assert D == 256 and A == 64 and NT == 32 and STEPS == 2 and NLC == 4

    with ExitStack() as ctx:
        def sb(name, shape, dt=F32):
            return ctx.enter_context(nc.sbuf_tensor(name, shape, dt))

        def sem(name):
            return ctx.enter_context(nc.semaphore(name))

        def scratch(name, shape, dt=F32):
            return nc.dram_tensor(name, shape, dt, kind="Internal").ap()

        q_s = scratch("q_s", (STEPS, NT, P, P))
        kh_s = scratch("kh_s", (NT, P, P))
        kl_s = scratch("kl_s", (NT, P, P))
        xa_s = scratch("xa_s", (NT, P, D))
        z_s = scratch("z_s", (NT, P, D))

        XA = sb("XA", [P, NT, W])
        XF = sb("XF", [P, NT, W])
        KH = sb("KH", [P, N], F32R)
        KL = sb("KL", [P, N], F32R)
        E = [sb(f"E{i}", [P, N]) for i in range(2)]
        M = [sb(f"M{i}", [P, N]) for i in range(2)]
        AT = sb("AT", [P, N])
        adj = sb("adj", [P, RING, PJ * P])
        sink = sb("sink", [P, N], U8)
        qt = sb("qt", [P, 2, P], F32R)
        ident = sb("ident", [P, P])
        wkq = sb("wkq", [P, 2, KT, P])
        gb = wkq[:, :, :, :].rearrange("p a k n -> p a (k n)")
        u1 = sb("u1", [P, KT, D])
        u2 = sb("u2", [P, KT, D])
        xa_t = sb("xa_t", [P, D])
        xf_t = sb("xf_t", [P, D])
        xT = sb("xT", [P, 2 * KT, P])
        z_t = sb("z_t", [P, D])
        x_t = sb("x_t", [P, D])
        y_t = sb("y_t", [P, D])
        hi_t = sb("hi_t", [P, 2, P], F32R)
        kl_t = sb("kl_t", [P, P], F32R)
        cand = sb("cand", [P, CANDS])
        order = sb("order", [P, 1 + DEPTH])
        before = sb("before", [P, 1 + DEPTH])
        spare = sb("spare", [P, DEPTH])
        flag_a = sb("flag_a", [P, 32])
        flag_b = sb("flag_b", [P, 32])

        def two(name, w=1):
            t = sb(name, [P, 2, w])
            return [t[:, i, :] for i in range(2)]

        cmax = two("cmax", NLC)
        negmax = two("negmax")
        total = two("total")
        target = two("target")
        rtotal = two("rtotal")
        nrtotal = two("nrtotal")
        thr = two("thr")
        nthr = two("nthr")
        rsum = two("rsum")
        ssum = two("ssum")
        frac = two("frac", 4)
        bits = two("bits", 4)
        power = two("power", 4)
        spread = two("spread")
        rtot4 = two("rtot4")
        kept = two("kept")
        small = sb("small", [P, 32])
        (cnt, gm, dz0, dz1, dd, hh, tt, below, below2, top8, estar, bad, tie, openr, take, res, negres, gab,
         ylim, al0, al1, rs, one, pbias, zero, anext, restie, anyf) = [small[:, i:i + 1] for i in range(28)]
        dz = small[:, 2:4]
        mv = sb("mv", [P, NT, 2])
        rstd = sb("rstd", [P, NT])
        nmr = sb("nmr", [P, NT])
        tmpn = sb("tmpn", [P, NT])
        stats = sb("stats", [P, 6])
        lo_bits = sb("lo_bits", [P, 1], I32)
        try_bits = sb("try_bits", [P, 1], I32)
        one_bit = sb("one_bit", [P, 1], I32)
        anyi = sb("anyi", [P, 1], I32)

        psL = ctx.enter_context(nc.psum_tensor("psL", [P, 2, LC], F32))
        psT = ctx.enter_context(nc.psum_tensor("psT", [P, 2, 512], F32))
        psR = ctx.enter_context(nc.psum_tensor("psR", [P, 512], F32))
        psA = ctx.enter_context(nc.psum_tensor("psA", [P, 512], F32))
        psT_all = psT[:, :, :].rearrange("p a n -> p (a n)")
        psX = psT[:, 0, :]
        psZ = psT[:, 1, 0:D]

        x_in = sem("x_in")
        weights_in = sem("weights_in")
        step_in = sem("step_in")
        step_u_in = sem("step_u_in")
        q_in = [sem(f"q_in{i}") for i in range(2)]
        adj_in = [sem(f"adj_in{i}") for i in range(RING)]
        tail_in = sem("tail_in")
        ident_zero = sem("ident_zero")
        ident_ready = sem("ident_ready")
        ones_ready = sem("ones_ready")
        norm_ready = sem("norm_ready")
        h_ready = sem("h_ready")
        fold_psum = sem("fold_psum")
        fold_ready = sem("fold_ready")
        first_xt_psum = sem("first_xt_psum")
        first_xt = sem("first_xt")
        first_kq_psum = sem("first_kq_psum")
        first_hi = sem("first_hi")
        first_lo = sem("first_lo")
        logits_ready = sem("logits_ready")
        logits_taken = sem("logits_taken")
        rowmax_ready = sem("rowmax_ready")
        exp_ready = sem("exp_ready")
        guess_ready = sem("guess_ready")
        sums_ready = sem("sums_ready")
        fracs_ready = sem("fracs_ready")
        powers_ready = sem("powers_ready")
        masked_ready = sem("masked_ready")
        block_ready = sem("block_ready")
        at_ready = sem("at_ready")
        adj_used = sem("adj_used")
        adj_taken = sem("adj_taken")
        attn_done = sem("attn_done")
        mixed_ready = sem("mixed_ready")
        xt_psum = sem("xt_psum")
        xt_ready = sem("xt_ready")
        z_psum = sem("z_psum")
        z_ready = sem("z_ready")
        kq_psum = sem("kq_psum")
        kq_ready = sem("kq_ready")
        y_ready = sem("y_ready")
        q_stored = sem("q_stored")
        kq_stored = sem("kq_stored")
        xa_stored = sem("xa_stored")
        z_stored = sem("z_stored")
        out_stored = sem("out_stored")

        ctx.enter_context(nc.allow_non_contiguous_dma(reason="rows of 512 bytes and more"))
        block = ctx.enter_context(nc.Block())

        GR = 2
        NG = NT // GR

        def sweep(eng, body):
            for n in range(STEPS):
                for t in (-1, 0, 1, 2, 3):
                    body(n, t, t % 2, (t + 1) // 2)
                with eng.Fori(2, NT // 2 - 1) as i:
                    body(n, 2 * i, 0, i)
                    body(n, 2 * i + 1, 1, i + 1)
                for t in (NT - 2, NT - 1, NT, NT + 1):
                    body(n, t, t % 2, (t + 1) // 2)

        def has(t, lag):
            return not isinstance(t, int) or 0 <= t - lag < NT

        @block.sync
        def _(sp):
            sp.dma_start(XF[:, :, 0:D], x_d.rearrange("t p d -> p t d")).then_inc(x_in, 16)
            sp.dma_start(wkq[:, 0, :, 0:A], w3t_d.rearrange("(k p) a -> p k a", p=P)).then_inc(weights_in, 16)
            sp.dma_start(wkq[:, 0, :, A:P], w3t_d.rearrange("(k p) a -> p k a", p=P)).then_inc(weights_in, 16)
            sp.dma_start(x_t[0:A, 0:D], w1_d[:, :]).then_inc(weights_in, 16)
            sp.dma_start(y_t[0:A, 0:A], w2t_d[:, :]).then_inc(weights_in, 16)
            sp.dma_start(y_t[0:A, A:P], w2t_d[:, :]).then_inc(weights_in, 16)
            sp.dma_start(u1[:], u1t_d[0].rearrange("(k p) n -> p k n", p=P)).then_inc(step_u_in, 16)
            sp.dma_start(u2[:], u2t_d[0].rearrange("(k p) n -> p k n", p=P)).then_inc(step_u_in, 16)
            with sp.Fori(0, NG) as g:
                sp.wait_ge(first_lo, g + 1)
                for j in range(GR):
                    sp.dma_start(q_s[0, g * GR + j], qt[:, j, :].bitcast(F32)).then_inc(q_stored, 16)

            def body(n, t, par, half):
                G = n * NT + t
                if n == 1 and isinstance(t, int) and t == -1:
                    sp.wait_ge(kq_stored, 48 * NT)
                    sp.wait_ge(xa_stored, 16 * NT)
                    sp.wait_ge(z_stored, 16 * NT)
                    sp.dma_start(KH[:, :].bitcast(F32).rearrange("p (t n) -> p t n", t=NT), kh_s.rearrange("t p n -> p t n")).then_inc(step_in, 16)
                    sp.dma_start(KL[:, :].bitcast(F32).rearrange("p (t n) -> p t n", t=NT), kl_s.rearrange("t p n -> p t n")).then_inc(step_in, 16)
                if has(t, -1):
                    if n == 0 and isinstance(t, int) and t == -1:
                        sp.wait_ge(q_stored, 16 * NT)
                    if not (n == 0 and isinstance(t, int) and t < 1):
                        sp.wait_ge(logits_ready, NLC * G)
                    q = (par + 1) % 2
                    sp.dma_start(qt[:, q, :].bitcast(F32), q_s[n, t + 1]).then_inc(q_in[q], 16)
                if n == 1 and isinstance(t, int) and t == -1:
                    sp.dma_start(XA[:, :, 0:D], xa_s.rearrange("t p d -> p t d")).then_inc(step_u_in, 16)
                    sp.dma_start(u1[:], u1t_d[1].rearrange("(k p) n -> p k n", p=P)).then_inc(step_u_in, 16)
                    sp.dma_start(u2[:], u2t_d[1].rearrange("(k p) n -> p k n", p=P)).then_inc(step_u_in, 16)
                    sp.dma_start(gb[:, 0, :], g_d[:, :]).then_inc(step_u_in, 16)
                    sp.dma_start(gb[:, 1, :], b_d[:, :]).then_inc(step_u_in, 16)
                if n == 1 and has(t, 2):
                    if not (isinstance(t, int) and t == 2):
                        sp.wait_ge(y_ready, t - 2)
                        sp.dma_start(out_d[t - 3], y_t[:]).then_inc(out_stored, 16)
                    sp.dma_start(x_t[:], x_d[t - 2]).then_inc(tail_in, 16)
                    sp.dma_start(z_t[:], z_s[t - 2]).then_inc(tail_in, 16)

                def pieces(i0, i1):
                    for i in range(i0, i1):
                        first = n == 0 and isinstance(t, int) and t == 1 and i < RING
                        if not first:
                            sp.wait_ge(adj_used, NPC * (G - 1) + i - RING + 1)
                        sp.dma_start(adj[:, i % RING, :], adj_d[t - 1, :, i * PJ * P:(i + 1) * PJ * P]).then_inc(adj_in[i % RING], 16)

                if has(t, 1):
                    pieces(0, RING)
                if has(t, 2) and n == 0:
                    sp.wait_ge(mixed_ready, G - 1)
                    sp.dma_start(xa_s[t - 2], xa_t[:]).then_inc(xa_stored, 16)
                    sp.wait_ge(z_ready, G - 1)
                    sp.dma_start(z_s[t - 2], z_t[:]).then_inc(z_stored, 16)
                    sp.wait_ge(kq_ready, G - 1)
                    sp.dma_start(kh_s[t - 2], hi_t[:, 0, :].bitcast(F32)).then_inc(kq_stored, 16)
                    sp.dma_start(kl_s[t - 2], kl_t[:].bitcast(F32)).then_inc(kq_stored, 16)
                    sp.dma_start(q_s[1, t - 2], hi_t[:, 1, :].bitcast(F32)).then_inc(kq_stored, 16)
                if has(t, 1):
                    pieces(RING, NPC)

            sweep(sp, body)
            sp.wait_ge(y_ready, NT)
            sp.dma_start(out_d[NT - 1], y_t[:]).then_inc(out_stored, 16)
            sp.wait_ge(out_stored, 16 * NT)
            sp.wait_ge(kq_stored, 48 * NT)

        @block.gpsimd
        def _(pool):
            nc.gpsimd.memset(ident[:], 0.0).then_inc(ident_zero, 1)
            pool.wait_ge(ident_zero, 1)
            nc.gpsimd.affine_select(out=ident[:], in_=ident[:], compare_op=ALU.not_equal, fill=1.0, base=0,
                                    pattern=[[-1, P]], channel_multiplier=1).then_inc(ident_ready, 1)

        @block.tensor
        def _(pe):
            pe.wait_ge(ident_ready, 1)
            pe.wait_ge(weights_in, 80)
            for k in range(KT):
                last = nc.tensor.matmul(psA[:, k * P:(k + 1) * P], x_t[0:A, k * P:(k + 1) * P], y_t[0:A, 0:P],
                                        start=True, stop=True)
            last.then_inc(fold_psum, 1)
            pe.wait_ge(fold_ready, 1)
            for g in range(NG):
                pe.wait_ge(h_ready, GR * (g + 1))
                if g >= 1:
                    pe.wait_ge(first_xt, g)
                for k in range(KT):
                    for j in range(GR):
                        last = nc.tensor.transpose(psX[:, (k * GR + j) * P:(k * GR + j + 1) * P],
                                                   XA[:, g * GR + j, k * P:(k + 1) * P], ident[:])
                last.then_inc(first_xt_psum, 1)
                pe.wait_ge(first_xt, g + 1)
                if g >= 1:
                    pe.wait_ge(first_lo, g)
                for w in range(2):
                    for k in range(KT):
                        last = nc.tensor.matmul(psT[:, 1, w * GR * P:(w + 1) * GR * P], wkq[:, w, k, :],
                                                AT[:, k * GR * P:(k + 1) * GR * P], start=(k == 0), stop=(k == KT - 1))
                last.then_inc(first_kq_psum, 1)

            def body(n, t, par, half):
                G = n * NT + t
                X_adj = XA if n == 0 else XF
                do_post = has(t, 2)
                g4 = G - 2

                def logits(c):
                    j = NLC * (G + 1) + c
                    if not (n == 0 and isinstance(t, int) and t == -1 and c < 2):
                        pe.wait_ge(logits_taken, j - 1)
                    for h in range(LC // 512):
                        lo = c * LC + h * 512
                        o = psL[:, c % 2, h * 512:(h + 1) * 512]
                        nc.tensor.matmul(o, qt[:, (par + 1) % 2, :], KH[:, lo:lo + 512], start=True, stop=False)
                        last = nc.tensor.matmul(o, qt[:, (par + 1) % 2, :], KL[:, lo:lo + 512], start=False, stop=True)
                    last.then_inc(logits_ready, 1)

                if has(t, -1):
                    if isinstance(t, int) and t == -1:
                        if n == 0:
                            pe.wait_ge(first_lo, NG)
                        else:
                            pe.wait_ge(step_in, 32)
                    pe.wait_ge(q_in[(par + 1) % 2], 16 * (n * NT // 2 + half + 1))
                    for c in range(NLC):
                        logits(c)

                g3 = G - 1

                def adjacency(q):
                    if not has(t, 1):
                        return
                    if q == 0:
                        if isinstance(t, int) and t == 1 and n == 1:
                            pe.wait_ge(step_u_in, 32 + 80)
                        if not (n == 0 and isinstance(t, int) and t == 1):
                            pe.wait_ge(adj_taken, g3)
                    for i in (2 * q, 2 * q + 1):
                        pe.wait_ge(adj_in[i % RING], 16 * (2 * g3 + i // RING + 1))
                        for j in range(PJ):
                            jt = i * PJ + j
                            last = nc.tensor.matmul(psR[:, 0:W], adj[:, i % RING, j * P:(j + 1) * P],
                                                    X_adj[:, jt, :], start=(jt == 0), stop=(jt == NT - 1))
                        last.then_inc(adj_used, 1)

                def transposes(q):
                    if q == 0:
                        pe.wait_ge(masked_ready, g3 + 1)
                        if do_post:
                            pe.wait_ge(z_ready, g4 + 1)
                            if n == 0:
                                pe.wait_ge(kq_ready, g4 + 1)
                    else:
                        pe.wait_ge(at_ready, 4 * g3 + q)
                    for b in range(8):
                        jt = 8 * q + b
                        last = nc.tensor.transpose(psT_all[:, b * P:(b + 1) * P],
                                                   M[(par + 1) % 2][:, jt * P:(jt + 1) * P], ident[:])
                    last.then_inc(block_ready, 1)

                def attention(q):
                    pe.wait_ge(at_ready, 4 * g3 + q + 1)
                    if q == 0 and not (n == 0 and isinstance(t, int) and t == 1):
                        pe.wait_ge(mixed_ready, g3)
                    for jt in range(8 * q, 8 * q + 8):
                        last = nc.tensor.matmul(psA[:, 0:D], AT[:, jt * P:(jt + 1) * P], XA[:, jt, 0:D],
                                                start=(jt == 0), stop=(jt == NT - 1))
                    if q == 3:
                        last.then_inc(attn_done, 1)

                adjacency(0)
                if do_post:
                    pe.wait_ge(mixed_ready, g4 + 1)
                    pe.wait_ge(at_ready, 4 * g4 + 4)
                    for s, src in ((0, xf_t), (1, xa_t)):
                        for k in range(KT):
                            b = s * KT + k
                            last = nc.tensor.transpose(psX[:, b * P:(b + 1) * P], src[:, k * P:(k + 1) * P], ident[:])
                    last.then_inc(xt_psum, 1)
                adjacency(1)
                if do_post:
                    if isinstance(t, int) and t == 2 and n == 0:
                        pe.wait_ge(step_u_in, 32)
                    pe.wait_ge(xt_ready, g4 + 1)
                    for s, u in ((0, u1), (1, u2)):
                        for k in range(KT):
                            last = nc.tensor.matmul(psZ, xT[:, s * KT + k, :], u[:, k, :],
                                                    start=(s + k == 0), stop=(s + k == KT))
                    last.then_inc(z_psum, 1)
                    if n == 0:
                        for w in range(2):
                            for k in range(KT):
                                last = nc.tensor.matmul(psX[:, w * P:(w + 1) * P], wkq[:, w, k, :], xT[:, KT + k, :],
                                                        start=(k == 0), stop=(k == KT - 1))
                        last.then_inc(kq_psum, 1)
                adjacency(2)
                if has(t, 1):
                    transposes(0)
                    transposes(1)
                    attention(0)
                    adjacency(3)
                    transposes(2)
                    attention(1)
                    transposes(3)
                    attention(2)
                    attention(3)

            sweep(pe, body)

        @block.scalar
        def _(act):
            act.wait_ge(norm_ready, 1)
            act.wait_ge(x_in, 16)
            for i in range(NT):
                nc.scalar.activation(XA[:, i, 0:D], XF[:, i, 0:D], ACT.Relu, bias=nmr[:, i:i + 1],
                                     scale=rstd[:, i:i + 1]).then_inc(h_ready, 1)
            def high_parts(g):
                act.wait_ge(first_kq_psum, g + 1)
                nc.scalar.copy(KH[:, bass.ds(g * GR * P, GR * P)], psT[:, 1, 0:GR * P])
                if not (isinstance(g, int) and g == 0):
                    act.wait_ge(q_stored, g * GR * 16)
                nc.scalar.copy(qt[:, :, :].rearrange("p a n -> p (a n)"), psT[:, 1, GR * P:2 * GR * P]).then_inc(first_hi, 1)

            high_parts(0)
            with act.Fori(1, NG) as g:
                high_parts(g)

            def body(n, t, par, half):
                G = n * NT + t

                def relu_sum(p, g, k):
                    act.drain()
                    act.wait_ge(guess_ready, EVALS * g + k + 1)
                    nc.scalar.activation(sink[:], E[p][:], ACT.Relu, bias=nthr[p], accum_out=rsum[p])

                def sign_sum(p):
                    act.drain()
                    nc.scalar.activation(sink[:], E[p][:], ACT.Sign, bias=nthr[p], accum_out=ssum[p]).then_inc(sums_ready, 1)

                def powers(p, g, k):
                    act.wait_ge(fracs_ready, EVALS * g + k + 1)
                    nc.scalar.activation(power[p], bits[p], ACT.Exp, bias=pbias,
                                         scale=QP * math.log(2) / 2 ** 23).then_inc(powers_ready, 1)

                def evacuate(q):
                    if has(t, 1):
                        act.wait_ge(block_ready, 4 * (G - 1) + q + 1)
                        nc.scalar.copy(AT[:, q * 1024:(q + 1) * 1024], psT_all).then_inc(at_ready, 1)

                if has(t, 0):
                    relu_sum(par, G, 2)
                    sign_sum(par)
                    powers(par, G, 2)
                p = (par + 1) % 2
                s1 = has(t, -1)
                if s1:
                    act.wait_ge(rowmax_ready, G + 2)
                    nc.scalar.activation(E[p][:], E[p][:], ACT.Exp, bias=negmax[p], accum_out=total[p]).then_inc(exp_ready, 1)
                    relu_sum(p, G + 1, 0)
                evacuate(0)
                if s1:
                    sign_sum(p)
                evacuate(1)
                if s1:
                    powers(p, G + 1, 0)
                    relu_sum(p, G + 1, 1)
                evacuate(2)
                if s1:
                    sign_sum(p)
                    powers(p, G + 1, 1)
                evacuate(3)

            sweep(act, body)

        @block.vector
        def _(v):
            V = nc.vector

            def fence():
                v.drain()

            def rsqrt(y, x, w):
                V.tensor_scalar(y.bitcast(I32), x.bitcast(I32), -0.5, float(0x5F3759DF), ALU.mult, ALU.add)
                for _ in range(4):
                    fence()
                    V.tensor_tensor(w, y, y, ALU.mult)
                    fence()
                    V.scalar_tensor_tensor(w, w, -0.5, x, ALU.mult, ALU.mult)
                    fence()
                    V.scalar_tensor_tensor(y, w, 1.5, y, ALU.add, ALU.mult)
                fence()

            V.memset(one, 1.0)
            V.memset(zero, 0.0)
            V.memset(pbias, -127.0 * QP * math.log(2) - math.log(QS) + 0.5 * math.log(RELAX))
            V.memset(flag_a[:], 0.0)
            V.memset(XA[:, :, D:W], 1.0)
            v.wait_ge(x_in, 16)
            V.memset(XF[:, :, D:W], 1.0)
            for i in range(NT):
                fence()
                V.bn_stats(stats[:], XF[:, i, 0:D])
                fence()
                V.bn_aggr(mv[:, i, :], stats[:])
            fence()
            V.tensor_scalar(nmr[:], mv[:, :, 1], LN_EPS, None, ALU.add)
            fence()
            rsqrt(rstd[:], nmr[:], tmpn[:])
            V.scalar_tensor_tensor(nmr[:], mv[:, :, 0], -1.0, rstd[:], ALU.mult, ALU.mult).then_inc(norm_ready, 1)
            v.wait_ge(fold_psum, 1)
            V.tensor_copy(wkq[:, 1, :, :].rearrange("p k n -> p (k n)"), psA[:, 0:KT * P]).then_inc(fold_ready, 1)
            with v.Fori(0, NG) as g:
                v.wait_ge(first_xt_psum, g + 1)
                V.tensor_copy(AT[:, 0:2 * GR * P], psX).then_inc(first_xt, 1)
                v.wait_ge(first_hi, g + 1)
                V.tensor_tensor(KL[:, bass.ds(g * GR * P, GR * P)], psT[:, 1, 0:GR * P],
                                KH[:, bass.ds(g * GR * P, GR * P)].bitcast(F32), ALU.subtract)
                ql = qt[A:P, :, :].rearrange("p a n -> p (a n)")
                V.tensor_tensor(ql, psT[A:P, 1, GR * P:2 * GR * P], ql.bitcast(F32), ALU.subtract).then_inc(first_lo, 1)

            def guess(p, n):
                a, b = GUESS[n]
                V.tensor_scalar(tt, total[p], b, None, ALU.add)
                fence()
                V.reciprocal(hh, tt)
                V.tensor_scalar(target[p], total[p], TOP_P, None, ALU.mult)
                fence()
                V.scalar_tensor_tensor(thr[p], total[p], a, hh, ALU.mult, ALU.mult)
                V.scalar_tensor_tensor(nthr[p], total[p], -a, hh, ALU.mult, ALU.mult).then_inc(guess_ready, 1)
                V.reciprocal(rtotal[p], total[p])
                fence()
                V.tensor_scalar(nrtotal[p], rtotal[p], -1.0, None, ALU.mult)

            def fractions(p, g, k, margin):
                fence()
                v.wait_ge(sums_ready, EVALS * g + k + 1)
                V.tensor_scalar(cnt, ssum[p], 0.5, N / 2 + margin, ALU.mult, ALU.add)
                V.tensor_scalar(frac[p][:, 0:1], ssum[p], 0.5 / N, 0.5, ALU.mult, ALU.add)
                V.tensor_scalar(frac[p][:, 2:3], ssum[p], -0.5 / N, 0.5, ALU.mult, ALU.add)
                fence()
                V.scalar_tensor_tensor(gm, cnt, thr[p], rsum[p], ALU.mult, ALU.add)
                fence()
                V.tensor_scalar(frac[p][:, 1:2], gm, rtotal[p], None, ALU.mult)
                V.tensor_scalar(frac[p][:, 3:4], gm, nrtotal[p], 1.0, ALU.mult, ALU.add)
                fence()
                V.tensor_scalar(bits[p], frac[p].bitcast(I32), float(107 << 23), None, ALU.max).then_inc(fracs_ready, 1)

            def advance(p):
                V.tensor_scalar(hh, dd, 0.5, 1.0, ALU.mult, ALU.add)
                fence()
                V.tensor_scalar(hh, hh, 0.5, 1.5, ALU.max, ALU.min)
                fence()
                V.scalar_tensor_tensor(thr[p], thr[p], hh, hh, ALU.mult, ALU.mult)
                fence()

            def update(p, g, k, last):
                v.wait_ge(powers_ready, EVALS * g + k + 1)
                V.tensor_tensor(dz, power[p][:, 0:2], power[p][:, 2:4], ALU.subtract)
                fence()
                V.tensor_tensor(spread[p], dz1, dz0, ALU.subtract)
                fence()
                V.scalar_tensor_tensor(dd, dz1, -quantile_of(TOP_P) * math.sqrt(RELAX), spread[p], ALU.add, ALU.mult)
                fence()
                V.tensor_scalar(hh, dd, 0.5, 1.0, ALU.mult, ALU.add)
                if last:
                    V.tensor_scalar(tt, cnt, FEW, 2.0, ALU.is_lt, ALU.mult)
                fence()
                V.tensor_scalar(hh, hh, 0.5, 1.5, ALU.max, ALU.min)
                fence()
                V.scalar_tensor_tensor(thr[p], thr[p], hh, hh, ALU.mult, ALU.mult)
                if last:
                    fence()
                    V.tensor_tensor(thr[p], thr[p], tt, ALU.add)
                else:
                    V.scalar_tensor_tensor(nthr[p], nthr[p], hh, hh, ALU.mult, ALU.mult).then_inc(guess_ready, 1)

            def list_below(p, half):
                c = slice(half * N // 2, (half + 1) * N // 2)
                V.scalar_tensor_tensor(M[p][:, c], E[p][:, c], thr[p], E[p][:, c], ALU.is_le, ALU.mult,
                                       accum_out=below2 if half else below)

            def segments(p):
                fence()
                V.scalar_tensor_tensor(order[:, 0:1], total[p], below, below2, ALU.subtract, ALU.subtract)
                for s in range(SEGS):
                    w = N // SEGS
                    V.max(cand[:, 8 * s:8 * s + 8], M[p][:, s * w:(s + 1) * w])
                fence()
                V.tensor_reduce(top8, cand[:, 7::8], AX, ALU.max)

            def rounds(r0, r1):
                for r in range(r0, r1):
                    V.max(order[:, 1 + 8 * r:9 + 8 * r], cand[:])
                    fence()
                    if r < ROUNDS - 1:
                        V.match_replace(cand[:], order[:, 1 + 8 * r:9 + 8 * r], cand[:], -1.0)
                        fence()

            def smallest_kept(p):
                V.tensor_tensor_scan(before[:], order[:], order[:], 0.0, ALU.add, ALU.max)
                V.tensor_tensor(bad, order[:, 0:1], target[p], ALU.is_ge)
                fence()
                V.tensor_scalar(spare[:], before[:, 0:DEPTH], target[p], 4.0, ALU.is_ge, ALU.mult)
                V.scalar_tensor_tensor(cand[:, 0:DEPTH], before[:, 0:DEPTH], target[p], order[:, 1:1 + DEPTH],
                                       ALU.is_ge, ALU.mult)
                V.scalar_tensor_tensor(bad, before[:, DEPTH - 1:DEPTH], target[p], bad, ALU.is_lt, ALU.add)
                fence()
                V.tensor_tensor(spare[:], spare[:], order[:, 1:1 + DEPTH], ALU.add)
                V.tensor_reduce(anext, cand[:, 0:DEPTH], AX, ALU.max)
                fence()
                V.tensor_reduce(estar, spare[:], AX, ALU.min)
                fence()
                V.scalar_tensor_tensor(bad, estar, top8, bad, ALU.is_le, ALU.add)
                V.tensor_tensor(tie, anext, estar, ALU.is_ge)

            def window(p):
                list_below(p, 0)
                list_below(p, 1)
                segments(p)
                rounds(0, ROUNDS)
                smallest_kept(p)

            def anyrow(flag):
                fence()
                V.tensor_copy(flag_a[:, 0:1], flag)
                fence()
                V.transpose(flag_b[:], flag_a[:])
                fence()
                V.tensor_reduce(anyf, flag_b[:], AX, ALU.max)
                fence()
                for q in range(4):
                    V.tensor_copy(flag_b[0:1, q:q + 1], anyf[32 * q:32 * q + 1, :])
                fence()
                V.tensor_reduce(anyi[0:1, 0:1], flag_b[0:1, 0:4], AX, ALU.max)
                fence()
                return V.value_load(anyi[0:1, 0:1], min_val=0, max_val=8)

            def keep(p, e):
                fence()
                V.scalar_tensor_tensor(M[p][:], E[p][:], e, E[p][:], ALU.is_ge, ALU.mult, accum_out=kept[p])

            def slow(p):
                V.tensor_scalar(openr, bad, 0.0, None, ALU.is_gt)
                V.tensor_copy(res, estar)
                V.tensor_copy(restie, tie)
                with v.Fori(0, REFINES) as _:
                    with v.If(anyrow(openr) > 0):
                        V.scalar_tensor_tensor(gm, thr[p], MARGIN, order[:, 0:1], ALU.mult, ALU.add)
                        fence()
                        V.tensor_scalar(gm, gm, rtotal[p], -TOP_P, ALU.mult, ALU.add)
                        fence()
                        V.scalar_tensor_tensor(dd, gm, 1.0 / (DENSITY * math.sqrt(RELAX)), spread[p], ALU.mult, ALU.mult)
                        fence()
                        advance(p)
                        window(p)
                        fence()
                        V.scalar_tensor_tensor(take, bad, 0.0, openr, ALU.is_equal, ALU.mult)
                        fence()
                        V.copy_predicated(res, take.bitcast(I32), estar)
                        V.copy_predicated(restie, take.bitcast(I32), tie)
                        V.tensor_tensor(openr, openr, take, ALU.subtract)
                    with v.Else():
                        v.nop()
                    v.nop()
                with v.If(anyrow(openr) > 0):
                    V.memset(lo_bits[:], 0)
                    V.memset(one_bit[:], 1 << 29)
                    with v.Fori(0, 30) as _:
                        fence()
                        V.tensor_tensor(try_bits[:], lo_bits[:], one_bit[:], ALU.bitwise_or)
                        fence()
                        V.tensor_scalar(one_bit[:], one_bit[:], 1, None, ALU.logical_shift_right)
                        V.scalar_tensor_tensor(M[p][:], E[p][:], try_bits[:].bitcast(F32), E[p][:], ALU.is_ge, ALU.mult,
                                               accum_out=gab)
                        fence()
                        V.tensor_tensor(take, gab, target[p], ALU.is_ge)
                        fence()
                        V.copy_predicated(lo_bits[:], take.bitcast(I32), try_bits[:])
                    fence()
                    V.copy_predicated(res, openr.bitcast(I32), lo_bits[:].bitcast(F32))
                    V.copy_predicated(restie, openr.bitcast(I32), one)
                with v.Else():
                    v.nop()
                v.nop()
                keep(p, res)
                with v.If(anyrow(restie) > 0):
                    V.scalar_tensor_tensor(M[p][:], E[p][:], res, E[p][:], ALU.is_gt, ALU.mult, accum_out=gab)
                    fence()
                    V.scalar_tensor_tensor(M[p][:], E[p][:], res, E[p][:], ALU.is_ge, ALU.mult)
                    V.tensor_tensor(gab, target[p], gab, ALU.subtract)
                    V.tensor_scalar(ylim, res, 1e-37, None, ALU.max)
                    V.tensor_scalar(negres, res, -1.0, None, ALU.mult)
                    fence()
                    V.reciprocal(ylim, ylim)
                    fence()
                    V.tensor_tensor(ylim, ylim, gab, ALU.mult)
                    V.tensor_scalar(E[p][:], M[p][:], res, None, ALU.is_equal)
                    fence()
                    V.tensor_scalar(ylim, ylim, 1.0, None, ALU.add)
                    V.tensor_tensor_scan(E[p][:], E[p][:], E[p][:], 0.0, ALU.add, ALU.max)
                    fence()
                    V.tensor_scalar(E[p][:], E[p][:], ylim, None, ALU.is_ge)
                    fence()
                    V.scalar_tensor_tensor(E[p][:], M[p][:], res, E[p][:], ALU.is_equal, ALU.mult)
                    fence()
                    V.scalar_tensor_tensor(M[p][:], E[p][:], negres, M[p][:], ALU.mult, ALU.add, accum_out=kept[p])
                with v.Else():
                    v.nop()
                v.nop()

            def body(n, t, par, half):
                G = n * NT + t
                X_adj = XA if n == 0 else XF
                p0, p1 = par, (par + 1) % 2
                s1, s2, s4 = has(t, -1), has(t, 0), has(t, 2)
                g4 = G - 2

                def take_logits(c):
                    v.wait_ge(logits_ready, NLC * (G + 1) + c + 1)
                    V.tensor_scalar(E[p1][:, c * LC:(c + 1) * LC], psL[:, c % 2, :], 0.0, None, ALU.add, ALU.max,
                                    accum_out=cmax[p1][:, c:c + 1]).then_inc(logits_taken, 1)

                if s4:
                    fence()
                    V.tensor_tensor(al0, kept[par], rtot4[par], ALU.mult)
                if s1:
                    for c in range(NLC):
                        take_logits(c)
                    fence()
                    V.tensor_reduce(negmax[p1], cmax[p1], AX, ALU.max)
                    fence()
                    V.tensor_scalar(negmax[p1], negmax[p1], -1.0, None, ALU.mult).then_inc(rowmax_ready, 1)
                if s4:
                    fence()
                    V.tensor_scalar(al0, al0, 1e-12, None, ALU.max)
                    fence()
                    V.reciprocal(al1, al0)
                    fence()
                    V.tensor_tensor(al1, al1, rtot4[par], ALU.mult)
                    fence()
                    v.wait_ge(attn_done, g4 + 1)
                    if n == 0 and not (isinstance(t, int) and t == 2):
                        v.wait_ge(xa_stored, 16 * (t - 2))
                    V.tensor_scalar(xa_t[:], psA[:, 0:D], al1, None, ALU.mult).then_inc(mixed_ready, 1)
                if s2:
                    fractions(p0, G, 2, MARGIN)
                if s4:
                    v.wait_ge(xt_psum, g4 + 1)
                    V.tensor_copy(xT[:, :, :].rearrange("p k n -> p (k n)"), psX).then_inc(xt_ready, 1)
                if s2:
                    update(p0, G, 2, True)
                    fence()
                    if not (n == 0 and isinstance(t, int) and t < 2):
                        v.wait_ge(block_ready, 4 * (G - 1))
                    list_below(p0, 0)
                if s1:
                    v.wait_ge(exp_ready, G + 2)
                    guess(p1, n)
                if s2:
                    list_below(p0, 1)
                if s4:
                    v.wait_ge(z_psum, g4 + 1)
                    if n == 0:
                        if not (isinstance(t, int) and t == 2):
                            v.wait_ge(z_stored, 16 * (t - 2))
                        V.tensor_tensor(z_t[:], psZ, XA[:, t - 2, 0:D], ALU.add).then_inc(z_ready, 1)
                    else:
                        v.wait_ge(tail_in, 32 * (t - 1))
                        V.tensor_tensor(z_t[:], psZ, z_t[:], ALU.add).then_inc(z_ready, 1)
                if s4 and n == 0:
                    v.wait_ge(kq_psum, g4 + 1)
                    if not (isinstance(t, int) and t == 2):
                        v.wait_ge(kq_stored, 48 * (t - 2))
                    V.tensor_copy(hi_t[:, :, :].rearrange("p a n -> p (a n)"), psX[:, 0:2 * P])
                    fence()
                    V.tensor_tensor(kl_t[:], psX[:, 0:P], hi_t[:, 0, :].bitcast(F32), ALU.subtract)
                    V.tensor_tensor(hi_t[A:P, 1, :], psX[A:P, P:2 * P], hi_t[A:P, 1, :].bitcast(F32),
                                    ALU.subtract).then_inc(kq_ready, 1)
                if s2:
                    segments(p0)
                if s1:
                    fractions(p1, G + 1, 0, 0.0)
                if s2:
                    rounds(0, 3)
                if s1:
                    update(p1, G + 1, 0, False)
                if s2:
                    fence()
                    rounds(3, ROUNDS)
                    smallest_kept(p0)
                    fence()
                    V.tensor_tensor(flag_a[:, 1:2], tie, bad, ALU.add)
                    keep(p0, estar)
                if s1:
                    fractions(p1, G + 1, 1, 0.0)
                if s2:
                    with v.If(anyrow(flag_a[:, 1:2]) > 0):
                        slow(p0)
                    with v.Else():
                        v.nop()
                    fence()
                    V.tensor_copy(rtot4[par], rtotal[par]).then_inc(masked_ready, 1)
                if s1:
                    update(p1, G + 1, 1, False)
                if has(t, 1):
                    fence()
                    v.wait_ge(adj_used, NPC * G)
                    V.tensor_scalar(rs, psR[:, D:W], 1.0, None, ALU.add)
                    V.scalar_tensor_tensor(xf_t[:], psR[:, 0:D], 1.0, X_adj[:, t - 1, 0:D], ALU.mult, ALU.add)
                    fence()
                    V.reciprocal(rs, rs)
                    fence()
                    last = V.tensor_scalar(xf_t[:], xf_t[:], rs, None, ALU.mult)
                    if n == 0:
                        fence()
                        last = V.tensor_copy(XF[:, t - 1, 0:D], xf_t[:])
                    last.then_inc(adj_taken, 1)
                if s4 and n == 1:
                    if isinstance(t, int) and t == 2:
                        v.wait_ge(step_u_in, 32 + 80)
                    fence()
                    V.bn_stats(stats[:], z_t[:])
                    fence()
                    V.bn_aggr(mv[:, 0, :], stats[:])
                    fence()
                    V.tensor_scalar(nmr[:, 0:1], mv[:, 0, 1:2], LN_EPS, None, ALU.add)
                    fence()
                    rsqrt(rstd[:, 0:1], nmr[:, 0:1], tmpn[:, 0:1])
                    if not (isinstance(t, int) and t == 2):
                        v.wait_ge(out_stored, 16 * (t - 2))
                    V.tensor_scalar(y_t[:], z_t[:], mv[:, 0, 0:1], rstd[:, 0:1], ALU.subtract, ALU.mult)
                    fence()
                    V.tensor_tensor(y_t[:], y_t[:], gb[:, 0, :], ALU.mult)
                    V.tensor_tensor(z_t[:], x_t[:], gb[:, 1, :], ALU.add)
                    fence()
                    V.tensor_tensor(y_t[:], y_t[:], z_t[:], ALU.add).then_inc(y_ready, 1)

            sweep(v, body)


def kernel(x, adj, L0_gnn_W1, L0_gnn_W2, L0_gnn_W3, L0_gnn_U1, L0_gnn_U2, L0_gnn_ln_g, L0_gnn_ln_b):
    import numpy as np
    import concourse.bacc as bacc
    from concourse.bass_utils import run_bass_kernel_spmd

    n, d = x.shape
    nt = n // P
    lay = np.ascontiguousarray
    arrays = {
        "x": lay(np.asarray(x).reshape(nt, P, d)),
        "adj": lay(np.asarray(adj).reshape(nt, P, nt, P).transpose(0, 3, 2, 1).reshape(nt, P, nt * P)),
        "w1": lay(np.asarray(L0_gnn_W1)),
        "w2t": lay(np.asarray(L0_gnn_W2).T),
        "w3t": lay(np.asarray(L0_gnn_W3).T),
        "u1t": lay(np.asarray(L0_gnn_U1).transpose(0, 2, 1)),
        "u2t": lay(np.asarray(L0_gnn_U2).transpose(0, 2, 1)),
        "ln_g": lay(np.broadcast_to(np.asarray(L0_gnn_ln_g), (P, d))),
        "ln_b": lay(np.broadcast_to(np.asarray(L0_gnn_ln_b), (P, d))),
    }
    nc = bacc.Bacc("TRN2", target_bir_lowering=False, num_devices=1)
    ins = [nc.dram_tensor(k + "_dram", a.shape, mybir.dt.from_np(a.dtype), kind="ExternalInput").ap() for k, a in arrays.items()]
    out = nc.dram_tensor("out", (nt, P, d), F32, kind="ExternalOutput").ap()
    adj_preln_kernel(nc, *ins, out)
    r = run_bass_kernel_spmd(nc, [{k + "_dram": a for k, a in arrays.items()}], core_ids=[0])
    return np.asarray(r.results[0]["out"]).reshape(n, d)
```

```python
from contextlib import ExitStack
import math

import concourse.bass as bass
from concourse import mybir
from concourse.alu_op_type import AluOpType as ALU

ACT = mybir.ActivationFunctionType
AX = mybir.AxisListType.X
F32 = mybir.dt.float32
F32R = mybir.dt.float32r
I32 = mybir.dt.int32
U8 = mybir.dt.uint8

P = 128
TOP_P = 0.9
LN_EPS = 1e-5

EVALS = 3
SEGS = 16
CANDS = 8 * SEGS
ROUNDS = 5
DEPTH = 8 * ROUNDS
MARGIN = 16.0
FEW = 36.0
RELAX = 0.82
QP = 0.135
QS = 0.1975
DENSITY = 0.1755
REFINES = 3
NEWTON = 3
GUESS = [(0.00537, 3.47), (0.526, 4096.0)]


def quantile_of(p):
    def power(x):
        e = math.floor(math.log2(x))
        return 2.0 ** (QP * (e + x / 2.0 ** e - 1.0))
    return (power(p) - power(1 - p)) / QS


def adj_preln_kernel(nc, x_d, adj_d, w1_d, w2t_d, w3t_d, u1t_d, u2t_d, g_d, b_d, out_d):
    NT, _, D = x_d.shape
    N = NT * P
    STEPS = u1t_d.shape[0]
    A = w1_d.shape[0]
    KT = D // P
    LC = 1024
    NLC = N // LC
    NPC = 8
    PJ = NT // NPC
    RING = 4
    W = D + 1
    assert D == 256 and A == 64 and NT == 32 and STEPS == 2 and NLC == 4

    with ExitStack() as ctx:
        def sb(name, shape, dt=F32):
            return ctx.enter_context(nc.sbuf_tensor(name, shape, dt))

        def sem(name):
            return ctx.enter_context(nc.semaphore(name))

        def scratch(name, shape, dt=F32):
            return nc.dram_tensor(name, shape, dt, kind="Internal").ap()

        q_s = scratch("q_s", (STEPS, NT, P, P))
        kh_s = scratch("kh_s", (NT, P, P))
        kl_s = scratch("kl_s", (NT, P, P))
        xa_s = scratch("xa_s", (NT, P, D))
        z_s = scratch("z_s", (NT, P, D))

        XA = sb("XA", [P, NT, W])
        XF = sb("XF", [P, NT, W])
        KH = sb("KH", [P, N], F32R)
        KL = sb("KL", [P, N], F32R)
        E = [sb(f"E{i}", [P, N]) for i in range(2)]
        M = [sb(f"M{i}", [P, N]) for i in range(2)]
        AT = sb("AT", [P, N])
        adj = sb("adj", [P, RING, PJ * P])
        sink = sb("sink", [P, N], U8)
        qt = sb("qt", [P, 2, P], F32R)
        ident = sb("ident", [P, P])
        wkq = sb("wkq", [P, 2, KT, P])
        gb = wkq[:, :, :, :].rearrange("p a k n -> p a (k n)")
        u1 = sb("u1", [P, KT, D])
        u2 = sb("u2", [P, KT, D])
        xa_t = sb("xa_t", [P, D])
        xf_t = sb("xf_t", [P, D])
        xT = sb("xT", [P, 2 * KT, P])
        z_t = sb("z_t", [P, D])
        x_t = sb("x_t", [P, D])
        y_t = sb("y_t", [P, D])
        hi_t = sb("hi_t", [P, 2, P], F32R)
        kl_t = sb("kl_t", [P, P], F32R)
        cand = sb("cand", [P, CANDS])
        order = sb("order", [P, 1 + DEPTH])
        before = sb("before", [P, 1 + DEPTH])
        spare = sb("spare", [P, DEPTH])
        flag_a = sb("flag_a", [P, 32])
        flag_b = sb("flag_b", [P, 32])

        def two(name, w=1):
            t = sb(name, [P, 2, w])
            return [t[:, i, :] for i in range(2)]

        cmax = two("cmax", NLC)
        negmax = two("negmax")
        total = two("total")
        target = two("target")
        rtotal = two("rtotal")
        nrtotal = two("nrtotal")
        thr = two("thr")
        nthr = two("nthr")
        rsum = two("rsum")
        ssum = two("ssum")
        frac = two("frac", 4)
        bits = two("bits", 4)
        power = two("power", 4)
        spread = two("spread")
        rtot4 = two("rtot4")
        kept = [two("kept0"), two("kept1")]
        small = sb("small", [P, 32])
        (cnt, gm, dz0, dz1, dd, hh, tt, below, below2, top8, estar, bad, tie, openr, take, res, gab, ylim,
          al0, al1, rs, one, pbias, zero, anext, restie) = [small[:, i:i + 1] for i in range(26)]
        anyf = small[:, 28:32]
        dz = small[:, 2:4]
        mv = sb("mv", [P, NT, 2])
        rstd = sb("rstd", [P, NT])
        nmr = sb("nmr", [P, NT])
        tmpn = sb("tmpn", [P, NT])
        stats = sb("stats", [P, 6])
        lo_bits = sb("lo_bits", [P, 1], I32)
        try_bits = sb("try_bits", [P, 1], I32)
        one_bit = sb("one_bit", [P, 1], I32)
        anyi = sb("anyi", [P, 1], I32)

        psL = ctx.enter_context(nc.psum_tensor("psL", [P, 2, LC], F32))
        psT = ctx.enter_context(nc.psum_tensor("psT", [P, 2, 512], F32))
        psR = ctx.enter_context(nc.psum_tensor("psR", [P, 512], F32))
        psA = ctx.enter_context(nc.psum_tensor("psA", [P, 512], F32))
        psT_all = psT[:, :, :].rearrange("p a n -> p (a n)")
        psX = psT[:, 0, :]
        psZ = psT[:, 1, 0:D]

        x_in = sem("x_in")
        weights_in = sem("weights_in")
        step_in = sem("step_in")
        step_u_in = sem("step_u_in")
        q_in = [sem(f"q_in{i}") for i in range(2)]
        adj_in = [sem(f"adj_in{i}") for i in range(RING)]
        tail_in = sem("tail_in")
        ident_zero = sem("ident_zero")
        ident_ready = sem("ident_ready")
        ones_ready = sem("ones_ready")
        norm_ready = sem("norm_ready")
        h_ready = sem("h_ready")
        fold_psum = sem("fold_psum")
        fold_ready = sem("fold_ready")
        first_xt_psum = sem("first_xt_psum")
        first_xt = sem("first_xt")
        first_kq_psum = sem("first_kq_psum")
        first_hi = sem("first_hi")
        first_lo = sem("first_lo")
        logits_ready = sem("logits_ready")
        logits_taken = sem("logits_taken")
        rowmax_ready = sem("rowmax_ready")
        exp_ready = sem("exp_ready")
        guess_ready = sem("guess_ready")
        sums_ready = sem("sums_ready")
        fracs_ready = sem("fracs_ready")
        powers_ready = sem("powers_ready")
        masked_ready = sem("masked_ready")
        block_ready = sem("block_ready")
        at_ready = sem("at_ready")
        adj_used = sem("adj_used")
        adj_taken = sem("adj_taken")
        attn_done = sem("attn_done")
        mixed_ready = sem("mixed_ready")
        xt_psum = sem("xt_psum")
        xt_ready = sem("xt_ready")
        z_psum = sem("z_psum")
        z_ready = sem("z_ready")
        kq_psum = sem("kq_psum")
        kq_ready = sem("kq_ready")
        y_ready = sem("y_ready")
        q_stored = sem("q_stored")
        kq_stored = sem("kq_stored")
        xa_stored = sem("xa_stored")
        z_stored = sem("z_stored")
        out_stored = sem("out_stored")

        ctx.enter_context(nc.allow_non_contiguous_dma(reason="rows of 512 bytes and more"))
        block = ctx.enter_context(nc.Block())

        GR = 2
        NG = NT // GR

        def sweep(eng, body):
            for n in range(STEPS):
                for t in (-1, 0, 1, 2, 3):
                    body(n, t, t % 2, (t + 1) // 2)
                with eng.Fori(2, NT // 2 - 1) as i:
                    body(n, 2 * i, 0, i)
                    body(n, 2 * i + 1, 1, i + 1)
                for t in (NT - 2, NT - 1, NT, NT + 1):
                    body(n, t, t % 2, (t + 1) // 2)

        def has(t, lag):
            return not isinstance(t, int) or 0 <= t - lag < NT

        @block.sync
        def _(sp):
            sp.dma_start(XF[:, :, 0:D], x_d.rearrange("t p d -> p t d")).then_inc(x_in, 16)
            sp.dma_start(wkq[:, 0, :, 0:A], w3t_d.rearrange("(k p) a -> p k a", p=P)).then_inc(weights_in, 16)
            sp.dma_start(wkq[:, 0, :, A:P], w3t_d.rearrange("(k p) a -> p k a", p=P)).then_inc(weights_in, 16)
            sp.dma_start(x_t[0:A, 0:D], w1_d[:, :]).then_inc(weights_in, 16)
            sp.dma_start(y_t[0:A, 0:A], w2t_d[:, :]).then_inc(weights_in, 16)
            sp.dma_start(y_t[0:A, A:P], w2t_d[:, :]).then_inc(weights_in, 16)
            sp.dma_start(u1[:], u1t_d[0].rearrange("(k p) n -> p k n", p=P)).then_inc(step_u_in, 16)
            sp.dma_start(u2[:], u2t_d[0].rearrange("(k p) n -> p k n", p=P)).then_inc(step_u_in, 16)
            with sp.Fori(0, NG) as g:
                sp.wait_ge(first_lo, g + 1)
                for j in range(GR):
                    sp.dma_start(q_s[0, g * GR + j], qt[:, j, :].bitcast(F32)).then_inc(q_stored, 16)

            def load_k(t0, t1):
                for k_sb, k_dram in ((KH, kh_s), (KL, kl_s)):
                    sp.dma_start(k_sb[:, t0 * P:t1 * P].bitcast(F32).rearrange("p (t n) -> p t n", t=t1 - t0),
                                 k_dram[t0:t1].rearrange("t p n -> p t n")).then_inc(step_in, 16)

            def body(n, t, par, half):
                G = n * NT + t
                if n == 0 and isinstance(t, int) and t == NT:
                    sp.wait_ge(kq_stored, 48 * (NT - 2))
                    sp.wait_ge(logits_ready, NLC * NT)
                    load_k(0, NT - 2)
                if n == 1 and isinstance(t, int) and t == -1:
                    sp.wait_ge(kq_stored, 48 * NT)
                    sp.wait_ge(xa_stored, 16 * NT)
                    sp.wait_ge(z_stored, 16 * NT)
                    load_k(NT - 2, NT)
                if has(t, -1):
                    if n == 0 and isinstance(t, int) and t == -1:
                        sp.wait_ge(q_stored, 16 * NT)
                    if not (n == 0 and isinstance(t, int) and t < 1):
                        sp.wait_ge(logits_ready, NLC * G)
                    q = (par + 1) % 2
                    sp.dma_start(qt[:, q, :].bitcast(F32), q_s[n, t + 1]).then_inc(q_in[q], 16)
                if n == 1 and isinstance(t, int) and t == -1:
                    sp.dma_start(XA[:, :, 0:D], xa_s.rearrange("t p d -> p t d")).then_inc(step_u_in, 16)
                    sp.dma_start(u1[:], u1t_d[1].rearrange("(k p) n -> p k n", p=P)).then_inc(step_u_in, 16)
                    sp.dma_start(u2[:], u2t_d[1].rearrange("(k p) n -> p k n", p=P)).then_inc(step_u_in, 16)
                    sp.dma_start(gb[:, 0, :], g_d[:, :]).then_inc(step_u_in, 16)
                    sp.dma_start(gb[:, 1, :], b_d[:, :]).then_inc(step_u_in, 16)
                if n == 1 and has(t, 2):
                    if not (isinstance(t, int) and t == 2):
                        sp.wait_ge(y_ready, t - 2)
                        sp.dma_start(out_d[t - 3], y_t[:]).then_inc(out_stored, 16)
                    sp.dma_start(x_t[:], x_d[t - 2]).then_inc(tail_in, 16)
                    sp.dma_start(z_t[:], z_s[t - 2]).then_inc(tail_in, 16)

                def pieces(i0, i1):
                    for i in range(i0, i1):
                        first = n == 0 and isinstance(t, int) and t == 1 and i < RING
                        if not first:
                            sp.wait_ge(adj_used, NPC * (G - 1) + i - RING + 1)
                        sp.dma_start(adj[:, i % RING, :], adj_d[t - 1, :, i * PJ * P:(i + 1) * PJ * P]).then_inc(adj_in[i % RING], 16)

                if has(t, 1):
                    pieces(0, NPC)
                if has(t, 2) and n == 0:
                    sp.wait_ge(mixed_ready, G - 1)
                    sp.dma_start(xa_s[t - 2], xa_t[:]).then_inc(xa_stored, 16)
                    sp.wait_ge(z_ready, G - 1)
                    sp.dma_start(z_s[t - 2], z_t[:]).then_inc(z_stored, 16)
                    sp.wait_ge(kq_ready, G - 1)
                    sp.dma_start(kh_s[t - 2], hi_t[:, 0, :].bitcast(F32)).then_inc(kq_stored, 16)
                    sp.dma_start(kl_s[t - 2], kl_t[:].bitcast(F32)).then_inc(kq_stored, 16)
                    sp.dma_start(q_s[1, t - 2], hi_t[:, 1, :].bitcast(F32)).then_inc(kq_stored, 16)

            sweep(sp, body)
            sp.wait_ge(y_ready, NT)
            sp.dma_start(out_d[NT - 1], y_t[:]).then_inc(out_stored, 16)
            sp.wait_ge(out_stored, 16 * NT)
            sp.wait_ge(kq_stored, 48 * NT)

        @block.gpsimd
        def _(pool):
            nc.gpsimd.memset(ident[:], 0.0).then_inc(ident_zero, 1)
            pool.wait_ge(ident_zero, 1)
            nc.gpsimd.affine_select(out=ident[:], in_=ident[:], compare_op=ALU.not_equal, fill=1.0, base=0,
                                    pattern=[[-1, P]], channel_multiplier=1).then_inc(ident_ready, 1)

        @block.tensor
        def _(pe):
            pe.wait_ge(ident_ready, 1)
            pe.wait_ge(weights_in, 80)
            for k in range(KT):
                last = nc.tensor.matmul(psA[:, k * P:(k + 1) * P], x_t[0:A, k * P:(k + 1) * P], y_t[0:A, 0:P],
                                        start=True, stop=True)
            last.then_inc(fold_psum, 1)
            pe.wait_ge(fold_ready, 1)
            for g in range(NG):
                pe.wait_ge(h_ready, GR * (g + 1))
                if g >= 1:
                    pe.wait_ge(first_xt, g)
                for k in range(KT):
                    for j in range(GR):
                        last = nc.tensor.transpose(psX[:, (k * GR + j) * P:(k * GR + j + 1) * P],
                                                   XA[:, g * GR + j, k * P:(k + 1) * P], ident[:])
                last.then_inc(first_xt_psum, 1)
                pe.wait_ge(first_xt, g + 1)
                if g >= 1:
                    pe.wait_ge(first_lo, g)
                for w in range(2):
                    for k in range(KT):
                        last = nc.tensor.matmul(psT[:, 1, w * GR * P:(w + 1) * GR * P], wkq[:, w, k, :],
                                                AT[:, k * GR * P:(k + 1) * GR * P], start=(k == 0), stop=(k == KT - 1))
                last.then_inc(first_kq_psum, 1)

            def body(n, t, par, half):
                G = n * NT + t
                X_adj = XA if n == 0 else XF
                do_post = has(t, 2)
                g4 = G - 2

                def logits(tile, q, c):
                    j = NLC * (n * NT + tile) + c
                    if not (n == 0 and isinstance(tile, int) and tile == 0 and c < 2):
                        pe.wait_ge(logits_taken, j - 1)
                    for h in range(LC // 512):
                        lo = c * LC + h * 512
                        o = psL[:, c % 2, h * 512:(h + 1) * 512]
                        nc.tensor.matmul(o, qt[:, q, :], KH[:, lo:lo + 512], start=True, stop=False)
                        last = nc.tensor.matmul(o, qt[:, q, :], KL[:, lo:lo + 512], start=False, stop=True)
                    last.then_inc(logits_ready, 1)

                if isinstance(t, int) and t == -1:
                    if n == 0:
                        pe.wait_ge(first_lo, NG)
                    else:
                        pe.wait_ge(step_in, 64)
                    pe.wait_ge(q_in[0], 16 * (n * NT // 2 + 1))
                    for c in range(NLC):
                        logits(0, 0, c)

                g3 = G - 1

                def adjacency(q):
                    if not has(t, 1):
                        return
                    if q == 0:
                        if isinstance(t, int) and t == 1 and n == 1:
                            pe.wait_ge(step_u_in, 32 + 80)
                            pe.wait_ge(mixed_ready, NT)
                        if not (n == 0 and isinstance(t, int) and t == 1):
                            pe.wait_ge(adj_taken, g3)
                    for i in (2 * q, 2 * q + 1):
                        pe.wait_ge(adj_in[i % RING], 16 * (2 * g3 + i // RING + 1))
                        for j in range(PJ):
                            jt = i * PJ + j
                            last = nc.tensor.matmul(psR[:, 0:W], adj[:, i % RING, j * P:(j + 1) * P],
                                                    X_adj[:, jt, :], start=(jt == 0), stop=(jt == NT - 1))
                        last.then_inc(adj_used, 1)

                def transposes(q):
                    if q == 0:
                        pe.wait_ge(masked_ready, g3 + 1)
                        if do_post:
                            pe.wait_ge(z_ready, g4 + 1)
                            if n == 0:
                                pe.wait_ge(kq_ready, g4 + 1)
                    else:
                        pe.wait_ge(at_ready, 4 * g3 + q)
                    for b in range(8):
                        jt = 8 * q + b
                        last = nc.tensor.transpose(psT_all[:, b * P:(b + 1) * P],
                                                   M[(par + 1) % 2][:, jt * P:(jt + 1) * P], ident[:])
                    last.then_inc(block_ready, 1)

                def attention(q, b0=0, b1=8):
                    if b0 == 0:
                        pe.wait_ge(at_ready, 4 * g3 + q + 1)
                    if q == 0 and not (n == 0 and isinstance(t, int) and t == 1):
                        pe.wait_ge(mixed_ready, g3)
                    for jt in range(8 * q + b0, 8 * q + b1):
                        last = nc.tensor.matmul(psA[:, 0:D], AT[:, jt * P:(jt + 1) * P], XA[:, jt, 0:D],
                                                start=(jt == 0), stop=(jt == NT - 1))
                    if jt == NT - 1:
                        last.then_inc(attn_done, 1)

                adjacency(0)
                if do_post:
                    pe.wait_ge(mixed_ready, g4 + 1)
                    pe.wait_ge(at_ready, 4 * g4 + 4)
                    for s in range(2):
                        for k in range(KT):
                            b, c = s * KT + k, slice(k * P, (k + 1) * P)
                            src = xa_t[:, c] if s else xf_t[:, c]
                            last = nc.tensor.transpose(psX[:, b * P:(b + 1) * P], src, ident[:])
                    last.then_inc(xt_psum, 1)
                adjacency(1)
                if do_post:
                    if isinstance(t, int) and t == 2 and n == 0:
                        pe.wait_ge(step_u_in, 32)
                    pe.wait_ge(xt_ready, g4 + 1)
                    for s, u in ((0, u1), (1, u2)):
                        for k in range(KT):
                            last = nc.tensor.matmul(psZ, xT[:, s * KT + k, :], u[:, k, :],
                                                    start=(s + k == 0), stop=(s + k == KT))
                    last.then_inc(z_psum, 1)
                    if n == 0:
                        for w in range(2):
                            for k in range(KT):
                                last = nc.tensor.matmul(psX[:, w * P:(w + 1) * P], wkq[:, w, k, :], xT[:, KT + k, :],
                                                        start=(k == 0), stop=(k == KT - 1))
                        last.then_inc(kq_psum, 1)
                adjacency(2)
                if has(t, 1):
                    transposes(0)
                    transposes(1)
                    attention(0)
                    transposes(2)
                    adjacency(3)
                    attention(1)
                    transposes(3)
                if has(t, -2):
                    pe.wait_ge(q_in[par], 16 * (n * NT // 2 + half + 2 - par))
                    logits(t + 2, par, 0)
                    logits(t + 2, par, 1)
                if has(t, 1):
                    attention(2)
                if has(t, -2):
                    logits(t + 2, par, 2)
                if has(t, 1):
                    attention(3, 0, 4)
                if has(t, -2):
                    logits(t + 2, par, 3)
                if has(t, 1):
                    attention(3, 4, 8)

            sweep(pe, body)

        @block.scalar
        def _(act):
            act.wait_ge(norm_ready, 1)
            act.wait_ge(x_in, 16)
            for i in range(NT):
                nc.scalar.activation(XA[:, i, 0:D], XF[:, i, 0:D], ACT.Relu, bias=nmr[:, i:i + 1],
                                     scale=rstd[:, i:i + 1]).then_inc(h_ready, 1)
            def high_parts(g):
                act.wait_ge(first_kq_psum, g + 1)
                nc.scalar.copy(KH[:, bass.ds(g * GR * P, GR * P)], psT[:, 1, 0:GR * P])
                if not (isinstance(g, int) and g == 0):
                    act.wait_ge(q_stored, g * GR * 16)
                nc.scalar.copy(qt[:, :, :].rearrange("p a n -> p (a n)"), psT[:, 1, GR * P:2 * GR * P]).then_inc(first_hi, 1)

            high_parts(0)
            with act.Fori(1, NG) as g:
                high_parts(g)

            def body(n, t, par, half):
                G = n * NT + t

                def relu_sum(p, g, k):
                    act.drain()
                    act.wait_ge(guess_ready, EVALS * g + k + 1)
                    nc.scalar.activation(sink[:], E[p][:], ACT.Relu, bias=nthr[p], accum_out=rsum[p])

                def sign_sum(p):
                    act.drain()
                    nc.scalar.activation(sink[:], E[p][:], ACT.Sign, bias=nthr[p], accum_out=ssum[p]).then_inc(sums_ready, 1)

                def powers(p, g, k):
                    act.wait_ge(fracs_ready, EVALS * g + k + 1)
                    nc.scalar.activation(power[p], bits[p], ACT.Exp, bias=pbias,
                                         scale=QP * math.log(2) / 2 ** 23).then_inc(powers_ready, 1)

                def evacuate(q):
                    if has(t, 1):
                        act.wait_ge(block_ready, 4 * (G - 1) + q + 1)
                        nc.scalar.copy(AT[:, q * 1024:(q + 1) * 1024], psT_all).then_inc(at_ready, 1)

                if has(t, 0):
                    relu_sum(par, G, 2)
                    sign_sum(par)
                    powers(par, G, 2)
                p = (par + 1) % 2
                s1 = has(t, -1)
                if s1:
                    act.wait_ge(rowmax_ready, G + 2)
                    nc.scalar.activation(E[p][:], E[p][:], ACT.Exp, bias=negmax[p], accum_out=total[p]).then_inc(exp_ready, 1)
                    relu_sum(p, G + 1, 0)
                    sign_sum(p)
                evacuate(0)
                if s1:
                    powers(p, G + 1, 0)
                evacuate(1)
                if s1:
                    relu_sum(p, G + 1, 1)
                evacuate(2)
                if s1:
                    sign_sum(p)
                    powers(p, G + 1, 1)
                evacuate(3)

            sweep(act, body)

        @block.vector
        def _(v):
            V = nc.vector

            def fence():
                v.drain()

            def rsqrt_guess(y, x):
                V.tensor_scalar(y.bitcast(I32), x.bitcast(I32), -0.5, float(0x5F3759DF), ALU.mult, ALU.add)

            def rsqrt(y, x, w):
                rsqrt_guess(y, x)
                for _ in range(NEWTON):
                    fence()
                    V.tensor_tensor(w, y, y, ALU.mult)
                    fence()
                    V.scalar_tensor_tensor(w, w, -0.5, x, ALU.mult, ALU.mult)
                    fence()
                    V.scalar_tensor_tensor(y, w, 1.5, y, ALU.add, ALU.mult)
                fence()

            V.memset(one, 1.0)
            V.memset(zero, 0.0)
            V.memset(pbias, -127.0 * QP * math.log(2) - math.log(QS) + 0.5 * math.log(RELAX))
            V.memset(flag_a[:], 0.0)
            V.memset(XA[:, :, D:W], 1.0)
            v.wait_ge(x_in, 16)
            V.memset(XF[:, :, D:W], 1.0)
            for i in range(NT):
                fence()
                V.bn_stats(stats[:], XF[:, i, 0:D])
                fence()
                V.bn_aggr(mv[:, i, :], stats[:])
            fence()
            V.tensor_scalar(nmr[:], mv[:, :, 1], LN_EPS, None, ALU.add)
            fence()
            rsqrt(rstd[:], nmr[:], tmpn[:])
            V.scalar_tensor_tensor(nmr[:], mv[:, :, 0], -1.0, rstd[:], ALU.mult, ALU.mult).then_inc(norm_ready, 1)
            v.wait_ge(fold_psum, 1)
            V.tensor_copy(wkq[:, 1, :, :].rearrange("p k n -> p (k n)"), psA[:, 0:KT * P]).then_inc(fold_ready, 1)
            with v.Fori(0, NG) as g:
                v.wait_ge(first_xt_psum, g + 1)
                V.tensor_copy(AT[:, 0:2 * GR * P], psX).then_inc(first_xt, 1)
                v.wait_ge(first_hi, g + 1)
                V.tensor_tensor(KL[:, bass.ds(g * GR * P, GR * P)], psT[:, 1, 0:GR * P],
                                KH[:, bass.ds(g * GR * P, GR * P)].bitcast(F32), ALU.subtract)
                ql = qt[A:P, :, :].rearrange("p a n -> p (a n)")
                V.tensor_tensor(ql, psT[A:P, 1, GR * P:2 * GR * P], ql.bitcast(F32), ALU.subtract).then_inc(first_lo, 1)

            def guess(p, n):
                a, b = GUESS[n]
                V.tensor_scalar(tt, total[p], b, None, ALU.add)
                fence()
                V.reciprocal(hh, tt)
                V.tensor_scalar(target[p], total[p], TOP_P, None, ALU.mult)
                fence()
                V.scalar_tensor_tensor(thr[p], total[p], a, hh, ALU.mult, ALU.mult)
                V.scalar_tensor_tensor(nthr[p], total[p], -a, hh, ALU.mult, ALU.mult).then_inc(guess_ready, 1)
                V.reciprocal(rtotal[p], total[p])
                fence()
                V.tensor_scalar(nrtotal[p], rtotal[p], -1.0, None, ALU.mult)

            def fractions(p, g, k, margin, flags=False):
                fence()
                if flags:
                    V.transpose(flag_b[:], flag_a[:])
                v.wait_ge(sums_ready, EVALS * g + k + 1)
                V.tensor_scalar(cnt, ssum[p], 0.5, N / 2 + margin, ALU.mult, ALU.add)
                V.tensor_scalar(frac[p][:, 0:1], ssum[p], 0.5 / N, 0.5, ALU.mult, ALU.add)
                V.tensor_scalar(frac[p][:, 2:3], ssum[p], -0.5 / N, 0.5, ALU.mult, ALU.add)
                fence()
                V.scalar_tensor_tensor(gm, cnt, thr[p], rsum[p], ALU.mult, ALU.add)
                if flags:
                    gather_blocks()
                fence()
                V.tensor_scalar(frac[p][:, 1:2], gm, rtotal[p], None, ALU.mult)
                V.tensor_scalar(frac[p][:, 3:4], gm, nrtotal[p], 1.0, ALU.mult, ALU.add)
                if flags:
                    gather_all()
                fence()
                V.tensor_scalar(bits[p], frac[p].bitcast(I32), float(107 << 23), None, ALU.max).then_inc(fracs_ready, 1)

            def advance(p):
                V.tensor_scalar(hh, dd, 0.5, 1.0, ALU.mult, ALU.add)
                fence()
                V.tensor_scalar(hh, hh, 0.5, 1.5, ALU.max, ALU.min)
                fence()
                V.scalar_tensor_tensor(thr[p], thr[p], hh, hh, ALU.mult, ALU.mult)
                fence()

            def update(p, g, k, last):
                v.wait_ge(powers_ready, EVALS * g + k + 1)
                V.tensor_tensor(dz, power[p][:, 0:2], power[p][:, 2:4], ALU.subtract)
                fence()
                V.tensor_tensor(spread[p], dz1, dz0, ALU.subtract)
                fence()
                V.scalar_tensor_tensor(dd, dz1, -quantile_of(TOP_P) * math.sqrt(RELAX), spread[p], ALU.add, ALU.mult)
                fence()
                V.tensor_scalar(hh, dd, 0.5, 1.0, ALU.mult, ALU.add)
                if last:
                    V.tensor_scalar(tt, cnt, FEW, 2.0, ALU.is_lt, ALU.mult)
                fence()
                V.tensor_scalar(hh, hh, 0.5, 1.5, ALU.max, ALU.min)
                fence()
                V.scalar_tensor_tensor(thr[p], thr[p], hh, hh, ALU.mult, ALU.mult)
                if last:
                    fence()
                    V.tensor_tensor(thr[p], thr[p], tt, ALU.add)
                else:
                    V.scalar_tensor_tensor(nthr[p], nthr[p], hh, hh, ALU.mult, ALU.mult).then_inc(guess_ready, 1)

            def list_below(p, half):
                c = slice(half * N // 2, (half + 1) * N // 2)
                V.scalar_tensor_tensor(M[p][:, c], E[p][:, c], thr[p], E[p][:, c], ALU.is_le, ALU.mult,
                                       accum_out=below2 if half else below)

            def segments(p, s0, s1):
                if s0 == 0:
                    fence()
                    V.scalar_tensor_tensor(order[:, 0:1], total[p], below, below2, ALU.subtract, ALU.subtract)
                for s in range(s0, s1):
                    w = N // SEGS
                    V.max(cand[:, 8 * s:8 * s + 8], M[p][:, s * w:(s + 1) * w])
                if s1 == SEGS:
                    fence()
                    V.tensor_reduce(top8, cand[:, 7::8], AX, ALU.max)

            def rounds(norm=False):
                for r in range(ROUNDS):
                    V.max(order[:, 1 + 8 * r:9 + 8 * r], cand[:])
                    if norm:
                        newton_step(2 * r)
                    fence()
                    if r < ROUNDS - 1:
                        V.match_replace(cand[:], order[:, 1 + 8 * r:9 + 8 * r], cand[:], -1.0)
                        if norm:
                            newton_step(2 * r + 1)
                        fence()

            def newton_step(i):
                y, x, w = rstd[:, 0:1], nmr[:, 0:1], tmpn[:, 0:1]
                if i % 3 == 0:
                    V.tensor_tensor(w, y, y, ALU.mult)
                elif i % 3 == 1:
                    V.scalar_tensor_tensor(w, w, -0.5, x, ALU.mult, ALU.mult)
                else:
                    V.scalar_tensor_tensor(y, w, 1.5, y, ALU.add, ALU.mult)

            def smallest_kept(p):
                V.tensor_tensor_scan(before[:], order[:], order[:], 0.0, ALU.add, ALU.max)
                V.tensor_tensor(bad, order[:, 0:1], target[p], ALU.is_ge)
                fence()
                V.scalar_tensor_tensor(spare[:], before[:, 0:DEPTH], target[p], order[:, 1:1 + DEPTH],
                                       ALU.is_ge, ALU.max)
                V.scalar_tensor_tensor(cand[:, 0:DEPTH], before[:, 0:DEPTH], target[p], order[:, 1:1 + DEPTH],
                                       ALU.is_ge, ALU.mult)
                V.scalar_tensor_tensor(bad, before[:, DEPTH - 1:DEPTH], target[p], bad, ALU.is_lt, ALU.add)
                fence()
                V.tensor_reduce(estar, spare[:], AX, ALU.min)
                V.tensor_reduce(anext, cand[:, 0:DEPTH], AX, ALU.max)
                fence()
                V.scalar_tensor_tensor(bad, estar, top8, bad, ALU.is_le, ALU.add)
                V.tensor_tensor(tie, anext, estar, ALU.is_ge)

            def window(p):
                list_below(p, 0)
                list_below(p, 1)
                segments(p, 0, SEGS)
                rounds()
                smallest_kept(p)

            def gather_flags():
                V.transpose(flag_b[:], flag_a[:])
                fence()
                gather_blocks()
                fence()
                gather_all()
                fence()

            def gather_blocks():
                for q in range(4):
                    V.tensor_reduce(anyf[0:1, q:q + 1], flag_b[32 * q:32 * q + 1, :], AX, ALU.max)

            def gather_all():
                V.tensor_reduce(anyi[0:1, 0:1], anyf[0:1, :], AX, ALU.max)

            def gathered():
                return V.value_load(anyi[0:1, 0:1], min_val=0, max_val=8)

            def anyof(flag):
                fence()
                V.tensor_copy(flag_a[:, 0:1], flag)
                fence()
                gather_flags()
                return gathered()

            def keep(p, e, half):
                c = slice(half * N // 2, (half + 1) * N // 2)
                V.scalar_tensor_tensor(M[p][:, c], E[p][:, c], e, E[p][:, c], ALU.is_ge, ALU.mult,
                                       accum_out=kept[half][p])

            def refine(p):
                V.scalar_tensor_tensor(gm, thr[p], MARGIN, order[:, 0:1], ALU.mult, ALU.add)
                fence()
                V.tensor_scalar(gm, gm, rtotal[p], -TOP_P, ALU.mult, ALU.add)
                fence()
                V.scalar_tensor_tensor(dd, gm, 1.0 / (DENSITY * math.sqrt(RELAX)), spread[p], ALU.mult, ALU.mult)
                fence()
                advance(p)
                window(p)
                fence()
                V.scalar_tensor_tensor(take, bad, 0.0, openr, ALU.is_equal, ALU.mult)
                fence()
                V.copy_predicated(res, take.bitcast(I32), estar)
                V.copy_predicated(restie, take.bitcast(I32), tie)
                V.tensor_tensor(openr, openr, take, ALU.subtract)

            def by_bits(p):
                V.memset(lo_bits[:], 0)
                V.memset(one_bit[:], 1 << 29)
                with v.Fori(0, 30) as _:
                    fence()
                    V.tensor_tensor(try_bits[:], lo_bits[:], one_bit[:], ALU.bitwise_or)
                    fence()
                    V.tensor_scalar(one_bit[:], one_bit[:], 1, None, ALU.logical_shift_right)
                    V.scalar_tensor_tensor(M[p][:], E[p][:], try_bits[:].bitcast(F32), E[p][:], ALU.is_ge, ALU.mult,
                                           accum_out=gab)
                    fence()
                    V.tensor_tensor(take, gab, target[p], ALU.is_ge)
                    fence()
                    V.copy_predicated(lo_bits[:], take.bitcast(I32), try_bits[:])
                fence()
                V.copy_predicated(res, openr.bitcast(I32), lo_bits[:].bitcast(F32))
                V.copy_predicated(restie, openr.bitcast(I32), one)

            def slow(p):
                V.tensor_scalar(openr, bad, 0.0, None, ALU.is_gt)
                V.tensor_copy(res, estar)
                V.tensor_copy(restie, tie)
                with v.If(anyof(openr) > 0):
                    refine(p)
                    with v.If(anyof(openr) > 0):
                        with v.Fori(0, REFINES - 1) as _:
                            with v.If(anyof(openr) > 0):
                                refine(p)
                            with v.Else():
                                v.nop()
                            v.nop()
                        with v.If(anyof(openr) > 0):
                            by_bits(p)
                        with v.Else():
                            v.nop()
                        v.nop()
                    with v.Else():
                        v.nop()
                    fence()
                    keep(p, res, 0)
                    keep(p, res, 1)
                with v.Else():
                    v.nop()
                with v.If(anyof(restie) > 0):
                    V.tensor_scalar(E[p][:], M[p][:], res, None, ALU.is_equal)
                    V.tensor_scalar(ylim, res, 1e-37, None, ALU.max)
                    V.tensor_tensor(gab, kept[0][p], kept[1][p], ALU.add)
                    fence()
                    V.tensor_tensor_scan(E[p][:], E[p][:], E[p][:], 0.0, ALU.add, ALU.max)
                    V.reciprocal(ylim, ylim)
                    V.tensor_tensor(gab, target[p], gab, ALU.subtract)
                    fence()
                    V.scalar_tensor_tensor(gab, E[p][:, N - 1:N], res, gab, ALU.mult, ALU.add)
                    fence()
                    V.tensor_tensor(ylim, ylim, gab, ALU.mult)
                    fence()
                    V.tensor_scalar(ylim, ylim, 1.0, None, ALU.add)
                    fence()
                    V.scalar_tensor_tensor(E[p][:], E[p][:], ylim, M[p][:], ALU.is_ge, ALU.mult)
                    fence()
                    V.scalar_tensor_tensor(M[p][:], E[p][:], res, M[p][:], ALU.not_equal, ALU.mult, accum_out=kept[0][p])
                    V.memset(kept[1][p], 0.0)
                with v.Else():
                    v.nop()
                v.nop()

            def body(n, t, par, half):
                G = n * NT + t
                X_adj = XA if n == 0 else XF
                p0, p1 = par, (par + 1) % 2
                s1, s2, s4 = has(t, -1), has(t, 0), has(t, 2)
                g4 = G - 2

                def take_logits(c):
                    v.wait_ge(logits_ready, NLC * (G + 1) + c + 1)
                    V.tensor_scalar(E[p1][:, c * LC:(c + 1) * LC], psL[:, c % 2, :], 0.0, None, ALU.add, ALU.max,
                                    accum_out=cmax[p1][:, c:c + 1]).then_inc(logits_taken, 1)

                if s4:
                    V.scalar_tensor_tensor(al0, kept[0][par], kept[1][par], rtot4[par], ALU.add, ALU.mult)
                    v.wait_ge(adj_used, NPC * (G - 1))
                    V.tensor_scalar(rs, psR[:, D:W], 1.0, None, ALU.add)
                    V.scalar_tensor_tensor(xf_t[:], psR[:, 0:D], 1.0, X_adj[:, t - 2, 0:D], ALU.mult, ALU.add)
                if s1:
                    take_logits(0)
                if s4:
                    fence()
                    V.tensor_scalar(al0, al0, 1e-12, None, ALU.max)
                    V.reciprocal(rs, rs)
                if s1:
                    take_logits(1)
                if s4:
                    fence()
                    V.tensor_scalar(xf_t[:], xf_t[:], rs, None, ALU.mult).then_inc(adj_taken, 1)
                    V.reciprocal(al1, al0)
                if s1:
                    take_logits(2)
                if s4:
                    fence()
                    V.tensor_tensor(al1, al1, rtot4[par], ALU.mult)
                    if n == 0:
                        V.tensor_copy(XF[:, t - 2, 0:D], xf_t[:])
                if s1:
                    take_logits(3)
                fence()
                if s1:
                    V.tensor_reduce(negmax[p1], cmax[p1], AX, ALU.max)
                    fence()
                    V.tensor_scalar(negmax[p1], negmax[p1], -1.0, None, ALU.mult).then_inc(rowmax_ready, 1)
                if s2:
                    fractions(p0, G, 2, MARGIN)
                if s4:
                    fence()
                    v.wait_ge(attn_done, g4 + 1)
                    if n == 0 and not (isinstance(t, int) and t == 2):
                        v.wait_ge(xa_stored, 16 * (t - 2))
                    V.tensor_scalar(xa_t[:], psA[:, 0:D], al1, None, ALU.mult).then_inc(mixed_ready, 1)
                if s2:
                    update(p0, G, 2, True)
                if s4:
                    v.wait_ge(xt_psum, g4 + 1)
                    V.tensor_copy(xT[:, :, :].rearrange("p k n -> p (k n)"), psX).then_inc(xt_ready, 1)
                if s2:
                    fence()
                    if not (n == 0 and isinstance(t, int) and t < 2):
                        v.wait_ge(block_ready, 4 * (G - 1))
                    list_below(p0, 0)
                if s1:
                    v.wait_ge(exp_ready, G + 2)
                    guess(p1, n)
                if s2:
                    list_below(p0, 1)
                if s4:
                    v.wait_ge(z_psum, g4 + 1)
                    if n == 0:
                        if not (isinstance(t, int) and t == 2):
                            v.wait_ge(z_stored, 16 * (t - 2))
                        V.tensor_tensor(z_t[:], psZ, XA[:, t - 2, 0:D], ALU.add).then_inc(z_ready, 1)
                    else:
                        v.wait_ge(tail_in, 32 * (t - 1))
                        V.tensor_tensor(z_t[:], psZ, z_t[:], ALU.add).then_inc(z_ready, 1)
                if s4 and n == 0:
                    v.wait_ge(kq_psum, g4 + 1)
                    if not (isinstance(t, int) and t == 2):
                        v.wait_ge(kq_stored, 48 * (t - 2))
                    V.tensor_copy(hi_t[:, :, :].rearrange("p a n -> p (a n)"), psX[:, 0:2 * P])
                    fence()
                    V.tensor_tensor(kl_t[:], psX[:, 0:P], hi_t[:, 0, :].bitcast(F32), ALU.subtract)
                    V.tensor_tensor(hi_t[A:P, 1, :], psX[A:P, P:2 * P], hi_t[A:P, 1, :].bitcast(F32),
                                    ALU.subtract).then_inc(kq_ready, 1)
                norm = s4 and n == 1
                if norm and isinstance(t, int) and t == 2:
                    v.wait_ge(step_u_in, 32 + 80)
                if s2:
                    segments(p0, 0, 12)
                elif norm:
                    fence()
                if norm:
                    V.bn_stats(stats[:], z_t[:])
                if s1:
                    fractions(p1, G + 1, 0, 0.0)
                else:
                    fence()
                if norm:
                    V.bn_aggr(mv[:, 0, :], stats[:])
                if s2:
                    segments(p0, 12, 14)
                if s1:
                    update(p1, G + 1, 0, False)
                else:
                    fence()
                if norm:
                    V.tensor_scalar(nmr[:, 0:1], mv[:, 0, 1:2], LN_EPS, None, ALU.add)
                if s2:
                    segments(p0, 14, SEGS)
                else:
                    fence()
                if norm:
                    rsqrt_guess(rstd[:, 0:1], nmr[:, 0:1])
                    fence()
                if s2:
                    rounds(norm)
                elif norm:
                    for i in range(3 * NEWTON):
                        newton_step(i)
                        fence()
                if norm:
                    if not (isinstance(t, int) and t == 2):
                        v.wait_ge(out_stored, 16 * (t - 2))
                    V.tensor_scalar(y_t[:], z_t[:], mv[:, 0, 0:1], rstd[:, 0:1], ALU.subtract, ALU.mult)
                if s2:
                    smallest_kept(p0)
                if norm:
                    fence()
                    V.tensor_tensor(y_t[:], y_t[:], gb[:, 0, :], ALU.mult)
                    V.tensor_tensor(z_t[:], x_t[:], gb[:, 1, :], ALU.add)
                if s2:
                    keep(p0, estar, 0)
                fence()
                if norm:
                    V.tensor_tensor(y_t[:], y_t[:], z_t[:], ALU.add).then_inc(y_ready, 1)
                if s2:
                    V.tensor_tensor(flag_a[:, 0:1], tie, bad, ALU.add)
                    keep(p0, estar, 1)
                if s1:
                    fractions(p1, G + 1, 1, 0.0, flags=s2)
                    update(p1, G + 1, 1, False)
                elif s2:
                    fence()
                    gather_flags()
                if s2:
                    with v.If(gathered() > 0):
                        slow(p0)
                    with v.Else():
                        v.nop()
                    fence()
                    V.tensor_copy(rtot4[par], rtotal[par]).then_inc(masked_ready, 1)

            sweep(v, body)


def kernel(x, adj, L0_gnn_W1, L0_gnn_W2, L0_gnn_W3, L0_gnn_U1, L0_gnn_U2, L0_gnn_ln_g, L0_gnn_ln_b):
    import numpy as np
    import concourse.bacc as bacc
    from concourse.bass_utils import run_bass_kernel_spmd

    n, d = x.shape
    nt = n // P
    lay = np.ascontiguousarray
    arrays = {
        "x": lay(np.asarray(x).reshape(nt, P, d)),
        "adj": lay(np.asarray(adj).reshape(nt, P, nt, P).transpose(0, 3, 2, 1).reshape(nt, P, nt * P)),
        "w1": lay(np.asarray(L0_gnn_W1)),
        "w2t": lay(np.asarray(L0_gnn_W2).T),
        "w3t": lay(np.asarray(L0_gnn_W3).T),
        "u1t": lay(np.asarray(L0_gnn_U1).transpose(0, 2, 1)),
        "u2t": lay(np.asarray(L0_gnn_U2).transpose(0, 2, 1)),
        "ln_g": lay(np.broadcast_to(np.asarray(L0_gnn_ln_g), (P, d))),
        "ln_b": lay(np.broadcast_to(np.asarray(L0_gnn_ln_b), (P, d))),
    }
    nc = bacc.Bacc("TRN2", target_bir_lowering=False, num_devices=1)
    ins = [nc.dram_tensor(k + "_dram", a.shape, mybir.dt.from_np(a.dtype), kind="ExternalInput").ap() for k, a in arrays.items()]
    out = nc.dram_tensor("out", (nt, P, d), F32, kind="ExternalOutput").ap()
    adj_preln_kernel(nc, *ins, out)
    r = run_bass_kernel_spmd(nc, [{k + "_dram": a for k, a in arrays.items()}], core_ids=[0])
    return np.asarray(r.results[0]["out"]).reshape(n, d)
```

```python
from contextlib import ExitStack
import math

import concourse.bass as bass
from concourse import mybir
from concourse.alu_op_type import AluOpType as ALU

ACT = mybir.ActivationFunctionType
AX = mybir.AxisListType.X
F32 = mybir.dt.float32
F32R = mybir.dt.float32r
I32 = mybir.dt.int32
U8 = mybir.dt.uint8

P = 128
TOP_P = 0.9
LN_EPS = 1e-5

EVALS = 3
SEGS = 16
CANDS = 8 * SEGS
ROUNDS = 5
DEPTH = 8 * ROUNDS
MARGIN = 16.0
FEW = 48.0
RELAX = 0.82
QP = 0.135
QS = 0.1975
DENSITY = 0.1755
REFINES = 3
OPEN = 4.0
NEWTON = 3
GUESS = [(0.00537, 3.47), (0.526, 4096.0)]


def quantile_of(p):
    def power(x):
        e = math.floor(math.log2(x))
        return 2.0 ** (QP * (e + x / 2.0 ** e - 1.0))
    return (power(p) - power(1 - p)) / QS


def adj_preln_kernel(nc, x_d, adj_d, w1_d, w2t_d, w3t_d, u1t_d, u2t_d, g_d, b_d, out_d):
    NT, _, D = x_d.shape
    N = NT * P
    STEPS = u1t_d.shape[0]
    A = w1_d.shape[0]
    KT = D // P
    LC = 1024
    NLC = N // LC
    NPC = 8
    PJ = NT // NPC
    RING = 4
    PARTS = 4
    PT = NT // PARTS
    GR = 4
    NG = NT // GR
    W = D + 1
    assert 3 * NEWTON == 2 * ROUNDS - 1
    assert D == 256 and A == 64 and NT == 32 and STEPS == 2 and NLC == 4

    with ExitStack() as ctx:
        def sb(name, shape, dt=F32):
            return ctx.enter_context(nc.sbuf_tensor(name, shape, dt))

        def sem(name):
            return ctx.enter_context(nc.semaphore(name))

        def scratch(name, shape, dt=F32):
            return nc.dram_tensor(name, shape, dt, kind="Internal").ap()

        q_s = scratch("q_s", (STEPS, NT, P, P))
        kh_s = scratch("kh_s", (NT, P, P))
        kl_s = scratch("kl_s", (NT, P, P))
        xa_s = scratch("xa_s", (NT, P, D))
        z_s = scratch("z_s", (NT, P, D))

        XA = sb("XA", [P, NT, W])
        XF = sb("XF", [P, NT, W])
        KH = sb("KH", [P, N], F32R)
        KL = sb("KL", [P, N], F32R)
        E = [sb(f"E{i}", [P, N]) for i in range(2)]
        M = [sb(f"M{i}", [P, N]) for i in range(2)]
        AT = sb("AT", [P, N])
        adj = sb("adj", [P, RING, PJ * P])
        sink = sb("sink", [P, N], U8)
        qt = sb("qt", [P, 2, P], F32R)
        ident = sb("ident", [P, P])
        wkq = sb("wkq", [P, 2, KT, P])
        gb = wkq[:, :, :, :].rearrange("p a k n -> p a (k n)")
        u1 = sb("u1", [P, KT, D])
        u2 = sb("u2", [P, KT, D])
        xa_t = sb("xa_t", [P, D])
        xf_t = sb("xf_t", [P, D])
        xT = sb("xT", [P, 2 * KT, P])
        z_t = sb("z_t", [P, D])
        x_t = sb("x_t", [P, D])
        y_t = sb("y_t", [P, D])
        hi_t = sb("hi_t", [P, 2, P], F32R)
        kl_t = sb("kl_t", [P, P], F32R)
        cand = sb("cand", [P, CANDS])
        order = sb("order", [P, 1 + DEPTH])
        before = sb("before", [P, 1 + DEPTH])
        spare = sb("spare", [P, DEPTH])
        flag_a = sb("flag_a", [P, 32])
        flag_b = sb("flag_b", [P, 32])

        def two(name, w=1):
            t = sb(name, [P, 2, w])
            return [t[:, i, :] for i in range(2)]

        cmin = two("cmin", NLC)
        negmax = two("negmax")
        total = two("total")
        target = two("target")
        rtotal = two("rtotal")
        nrtotal = two("nrtotal")
        thr = two("thr")
        nthr = two("nthr")
        rsum = two("rsum")
        ssum = two("ssum")
        frac = two("frac", 4)
        bits = two("bits", 4)
        power = two("power", 4)
        spread = two("spread")
        rtot4 = two("rtot4")
        kept = [two("kept0"), two("kept1")]
        small = sb("small", [P, 32])
        (cnt, gm, dz0, dz1, dd, hh, tt, below, below2, top8, estar, bad, tie, openr, take, res, gab, ylim,
         al0, al1, rs, one, pbias, anext, restie) = [small[:, i:i + 1] for i in range(25)]
        anyf = small[:, 28:32]
        dz = small[:, 2:4]
        mv = sb("mv", [P, NT, 2])
        rstd = sb("rstd", [P, NT])
        nmr = sb("nmr", [P, NT])
        tmpn = sb("tmpn", [P, NT])
        stats = sb("stats", [P, 6])
        lo_bits = sb("lo_bits", [P, 1], I32)
        try_bits = sb("try_bits", [P, 1], I32)
        one_bit = sb("one_bit", [P, 1], I32)
        anyi = sb("anyi", [P, 1], I32)

        psL = ctx.enter_context(nc.psum_tensor("psL", [P, 2, LC], F32))
        psT = ctx.enter_context(nc.psum_tensor("psT", [P, 2, 512], F32))
        psR = ctx.enter_context(nc.psum_tensor("psR", [P, 512], F32))
        psA = ctx.enter_context(nc.psum_tensor("psA", [P, 512], F32))
        psT_all = psT[:, :, :].rearrange("p a n -> p (a n)")
        psX = psT[:, 0, :]
        psZ = psT[:, 1, 0:D]

        x_in = [sem(f"x_in{i}") for i in range(PARTS)]
        weights_in = sem("weights_in")
        step_in = sem("step_in")
        step_u_in = sem("step_u_in")
        q_in = [sem(f"q_in{i}") for i in range(2)]
        adj_in = [sem(f"adj_in{i}") for i in range(RING)]
        tail_in = sem("tail_in")
        ident_zero = sem("ident_zero")
        ident_ready = sem("ident_ready")
        ones_ready = sem("ones_ready")
        norm_ready = sem("norm_ready")
        h_ready = sem("h_ready")
        fold_psum = sem("fold_psum")
        fold_ready = sem("fold_ready")
        first_xt_psum = sem("first_xt_psum")
        first_xt = sem("first_xt")
        first_kq_psum = sem("first_kq_psum")
        first_hi = sem("first_hi")
        first_lo = sem("first_lo")
        logits_ready = sem("logits_ready")
        logits_taken = sem("logits_taken")
        rowmax_ready = sem("rowmax_ready")
        exp_ready = sem("exp_ready")
        guess_ready = sem("guess_ready")
        sums_ready = sem("sums_ready")
        fracs_ready = sem("fracs_ready")
        powers_ready = sem("powers_ready")
        masked_ready = sem("masked_ready")
        block_ready = sem("block_ready")
        at_ready = sem("at_ready")
        adj_used = sem("adj_used")
        scales_ready = sem("scales_ready")
        adj_taken = sem("adj_taken")
        attn_done = sem("attn_done")
        mixed_ready = sem("mixed_ready")
        xt_psum = sem("xt_psum")
        xt_ready = sem("xt_ready")
        z_psum = sem("z_psum")
        z_ready = sem("z_ready")
        kq_psum = sem("kq_psum")
        kq_ready = sem("kq_ready")
        y_normed = sem("y_normed")
        xb_ready = sem("xb_ready")
        yg_ready = sem("yg_ready")
        y_ready = sem("y_ready")
        q_stored = sem("q_stored")
        kq_stored = sem("kq_stored")
        xa_stored = sem("xa_stored")
        z_stored = sem("z_stored")
        out_stored = sem("out_stored")

        ctx.enter_context(nc.allow_non_contiguous_dma(reason="rows of 512 bytes and more"))
        block = ctx.enter_context(nc.Block())


        first_xt_ps = [psL[:, 0, :], psT_all]
        first_k_ps = [psL[:, 1, 0:512], psR[:, :]]
        first_q_ps = [psL[:, 1, 512:1024], psA[:, :]]

        def group(g):
            return slice(g * GR * P, (g + 1) * GR * P)

        def sweep(eng, body):
            for n in range(STEPS):
                for t in (-1, 0, 1, 2, 3):
                    body(n, t, t % 2, (t + 1) // 2)
                with eng.Fori(2, NT // 2 - 1) as i:
                    body(n, 2 * i, 0, i)
                    body(n, 2 * i + 1, 1, i + 1)
                for t in (NT - 2, NT - 1, NT, NT + 1):
                    body(n, t, t % 2, (t + 1) // 2)

        def has(t, lag):
            return not isinstance(t, int) or 0 <= t - lag < NT

        @block.sync
        def _(sp):
            sp.dma_start(wkq[:, 0, :, 0:A], w3t_d.rearrange("(k p) a -> p k a", p=P)).then_inc(weights_in, 16)
            sp.dma_start(wkq[:, 0, :, A:P], w3t_d.rearrange("(k p) a -> p k a", p=P)).then_inc(weights_in, 16)
            sp.dma_start(x_t[0:A, 0:D], w1_d[:, :]).then_inc(weights_in, 16)
            sp.dma_start(y_t[0:A, 0:A], w2t_d[:, :]).then_inc(weights_in, 16)
            sp.dma_start(y_t[0:A, A:P], w2t_d[:, :]).then_inc(weights_in, 16)
            for i in range(PARTS):
                sp.dma_start(XF[:, i * PT:(i + 1) * PT, 0:D],
                             x_d[i * PT:(i + 1) * PT].rearrange("t p d -> p t d")).then_inc(x_in[i], 16)
            sp.dma_start(u1[:], u1t_d[0].rearrange("(k p) n -> p k n", p=P)).then_inc(step_u_in, 16)
            sp.dma_start(u2[:], u2t_d[0].rearrange("(k p) n -> p k n", p=P)).then_inc(step_u_in, 16)
            for g in range(NG):
                sp.wait_ge(first_lo, g + 1)
                sp.dma_start(q_s[0, g * GR:(g + 1) * GR].rearrange("t p n -> p t n"),
                             M[0][:, g * GR * P:(g + 1) * GR * P].rearrange("p (t n) -> p t n", t=GR)).then_inc(q_stored, 16)

            def load_k(t0, t1):
                for k_sb, k_dram in ((KH, kh_s), (KL, kl_s)):
                    sp.dma_start(k_sb[:, t0 * P:t1 * P].bitcast(F32).rearrange("p (t n) -> p t n", t=t1 - t0),
                                 k_dram[t0:t1].rearrange("t p n -> p t n")).then_inc(step_in, 16)

            def body(n, t, par, half):
                G = n * NT + t
                if n == 0 and isinstance(t, int) and t == NT:
                    sp.wait_ge(kq_stored, 48 * (NT - 2))
                    sp.wait_ge(logits_ready, NLC * NT)
                    load_k(0, NT - 2)
                if n == 1 and isinstance(t, int) and t == -1:
                    sp.wait_ge(kq_stored, 48 * NT)
                    sp.wait_ge(xa_stored, 16 * NT)
                    sp.wait_ge(z_stored, 16 * NT)
                    load_k(NT - 2, NT)
                if has(t, -1):
                    if n == 0 and isinstance(t, int) and t == -1:
                        sp.wait_ge(q_stored, 16 * NG)
                    if not (n == 0 and isinstance(t, int) and t < 1):
                        sp.wait_ge(logits_ready, NLC * G)
                    q = (par + 1) % 2
                    sp.dma_start(qt[:, q, :].bitcast(F32), q_s[n, t + 1]).then_inc(q_in[q], 16)
                if n == 1 and isinstance(t, int) and t == -1:
                    sp.dma_start(XA[:, :, 0:D], xa_s.rearrange("t p d -> p t d")).then_inc(step_u_in, 16)
                    sp.dma_start(u1[:], u1t_d[1].rearrange("(k p) n -> p k n", p=P)).then_inc(step_u_in, 16)
                    sp.dma_start(u2[:], u2t_d[1].rearrange("(k p) n -> p k n", p=P)).then_inc(step_u_in, 16)
                    sp.dma_start(gb[:, 0, :], g_d[:, :]).then_inc(step_u_in, 16)
                    sp.dma_start(gb[:, 1, :], b_d[:, :]).then_inc(step_u_in, 16)
                if n == 1 and has(t, 2):
                    if not (isinstance(t, int) and t == 2):
                        sp.wait_ge(y_ready, t - 2)
                        sp.dma_start(out_d[t - 3], y_t[:]).then_inc(out_stored, 16)
                    sp.dma_start(x_t[:], x_d[t - 2]).then_inc(tail_in, 16)
                    sp.dma_start(z_t[:], z_s[t - 2]).then_inc(tail_in, 16)

                def pieces(i0, i1):
                    for i in range(i0, i1):
                        first = n == 0 and isinstance(t, int) and t == 1 and i < RING
                        if not first:
                            sp.wait_ge(adj_used, NPC * (G - 1) + i - RING + 1)
                        sp.dma_start(adj[:, i % RING, :], adj_d[t - 1, :, i * PJ * P:(i + 1) * PJ * P]).then_inc(adj_in[i % RING], 16)

                if has(t, 1):
                    pieces(0, NPC)
                if has(t, 2) and n == 0:
                    sp.wait_ge(mixed_ready, G - 1)
                    sp.dma_start(xa_s[t - 2], xa_t[:]).then_inc(xa_stored, 16)
                    sp.wait_ge(z_ready, G - 1)
                    sp.dma_start(z_s[t - 2], z_t[:]).then_inc(z_stored, 16)
                    sp.wait_ge(kq_ready, G - 1)
                    sp.dma_start(kh_s[t - 2], hi_t[:, 0, :].bitcast(F32)).then_inc(kq_stored, 16)
                    sp.dma_start(kl_s[t - 2], kl_t[:].bitcast(F32)).then_inc(kq_stored, 16)
                    sp.dma_start(q_s[1, t - 2], hi_t[:, 1, :].bitcast(F32)).then_inc(kq_stored, 16)

            sweep(sp, body)
            sp.wait_ge(y_ready, NT)
            sp.dma_start(out_d[NT - 1], y_t[:]).then_inc(out_stored, 16)
            sp.wait_ge(out_stored, 16 * NT)
            sp.wait_ge(kq_stored, 48 * NT)

        @block.gpsimd
        def _(pool):
            nc.gpsimd.memset(ident[:], 0.0).then_inc(ident_zero, 1)
            pool.wait_ge(ident_zero, 1)
            nc.gpsimd.affine_select(out=ident[:], in_=ident[:], compare_op=ALU.not_equal, fill=1.0, base=0,
                                    pattern=[[-1, P]], channel_multiplier=1).then_inc(ident_ready, 1)
            with pool.Fori(0, NT) as i:
                pool.wait_ge(y_normed, i + 1)
                nc.gpsimd.tensor_tensor(z_t[:], x_t[:], gb[:, 1, :], ALU.add).then_inc(xb_ready, 1)
                nc.gpsimd.tensor_tensor(y_t[:], y_t[:], gb[:, 0, :], ALU.mult).then_inc(yg_ready, 1)
                pool.wait_ge(xb_ready, i + 1)
                pool.wait_ge(yg_ready, i + 1)
                nc.gpsimd.tensor_tensor(y_t[:], y_t[:], z_t[:], ALU.add).then_inc(y_ready, 1)

        @block.tensor
        def _(pe):
            pe.wait_ge(ident_ready, 1)
            pe.wait_ge(weights_in, 80)
            for k in range(KT):
                last = nc.tensor.matmul(psA[:, k * P:(k + 1) * P], x_t[0:A, k * P:(k + 1) * P], y_t[0:A, 0:P],
                                        start=True, stop=True)
            last.then_inc(fold_psum, 1)
            pe.wait_ge(fold_ready, 1)
            def first_transposes(g):
                pe.wait_ge(h_ready, GR * (g + 1))
                if g >= 2:
                    pe.wait_ge(first_xt, g - 1)
                for k in range(KT):
                    for j in range(GR):
                        last = nc.tensor.transpose(first_xt_ps[g % 2][:, (k * GR + j) * P:(k * GR + j + 1) * P],
                                                   XA[:, g * GR + j, k * P:(k + 1) * P], ident[:])
                last.then_inc(first_xt_psum, 1)

            first_transposes(0)
            for g in range(NG):
                if g + 1 < NG:
                    first_transposes(g + 1)
                pe.wait_ge(first_xt, g + 1)
                if g >= 2:
                    pe.wait_ge(first_lo, g - 1)
                for w, o in ((0, first_k_ps[g % 2]), (1, first_q_ps[g % 2])):
                    for k in range(KT):
                        a0 = (g % 2 * KT + k) * GR * P
                        last = nc.tensor.matmul(o, wkq[:, w, k, :], AT[:, a0:a0 + GR * P],
                                                start=(k == 0), stop=(k == KT - 1))
                last.then_inc(first_kq_psum, 1)

            def body(n, t, par, half):
                G = n * NT + t
                X_adj = XA if n == 0 else XF
                do_post = has(t, 2)
                g4 = G - 2

                def logits(tile, q, c):
                    j = NLC * (n * NT + tile) + c
                    if not (n == 0 and isinstance(tile, int) and tile == 0 and c < 2):
                        pe.wait_ge(logits_taken, j - 1)
                    for h in range(LC // 512):
                        lo = c * LC + h * 512
                        o = psL[:, c % 2, h * 512:(h + 1) * 512]
                        nc.tensor.matmul(o, qt[:, q, :], KH[:, lo:lo + 512], start=True, stop=False)
                        last = nc.tensor.matmul(o, qt[:, q, :], KL[:, lo:lo + 512], start=False, stop=True)
                    last.then_inc(logits_ready, 1)

                if isinstance(t, int) and t == -1:
                    if n == 0:
                        pe.wait_ge(first_lo, NG)
                    else:
                        pe.wait_ge(step_in, 64)
                    pe.wait_ge(q_in[0], 16 * (n * NT // 2 + 1))
                    for c in range(NLC):
                        logits(0, 0, c)

                g3 = G - 1

                def adjacency(i0, i1):
                    if not has(t, 1):
                        return
                    if i0 == 0:
                        if isinstance(t, int) and t == 1 and n == 1:
                            pe.wait_ge(step_u_in, 32 + 80)
                            pe.wait_ge(mixed_ready, NT)
                        if not (n == 0 and isinstance(t, int) and t == 1):
                            pe.wait_ge(adj_taken, g3)
                        nc.tensor.matmul(psR[:, 0:W], ident[:], X_adj[:, t - 1, :], start=True, stop=False)
                    for i in range(i0, i1):
                        pe.wait_ge(adj_in[i % RING], 16 * (2 * g3 + i // RING + 1))
                        for j in range(PJ):
                            jt = i * PJ + j
                            last = nc.tensor.matmul(psR[:, 0:W], adj[:, i % RING, j * P:(j + 1) * P],
                                                    X_adj[:, jt, :], start=False, stop=(jt == NT - 1))
                        last.then_inc(adj_used, 1)

                def transposes(q):
                    if q == 0:
                        pe.wait_ge(masked_ready, g3 + 1)
                        if do_post:
                            pe.wait_ge(z_ready, g4 + 1)
                            if n == 0:
                                pe.wait_ge(kq_ready, g4 + 1)
                    else:
                        pe.wait_ge(at_ready, 4 * g3 + q)
                    for b in range(8):
                        jt = 8 * q + b
                        last = nc.tensor.transpose(psT_all[:, b * P:(b + 1) * P],
                                                   M[(par + 1) % 2][:, jt * P:(jt + 1) * P], ident[:])
                    last.then_inc(block_ready, 1)

                def attention(q, b0=0, b1=8):
                    if b0 == 0:
                        pe.wait_ge(at_ready, 4 * g3 + q + 1)
                    if q == 0 and not (n == 0 and isinstance(t, int) and t == 1):
                        pe.wait_ge(mixed_ready, g3)
                    for jt in range(8 * q + b0, 8 * q + b1):
                        last = nc.tensor.matmul(psA[:, 0:D], AT[:, jt * P:(jt + 1) * P], XA[:, jt, 0:D],
                                                start=(jt == 0), stop=(jt == NT - 1))
                    if jt == NT - 1:
                        last.then_inc(attn_done, 1)

                adjacency(0, 2)
                if do_post:
                    pe.wait_ge(mixed_ready, g4 + 1)
                    pe.wait_ge(at_ready, 4 * g4 + 4)
                    for s in range(2):
                        for k in range(KT):
                            b, c = s * KT + k, slice(k * P, (k + 1) * P)
                            src = xa_t[:, c] if s else xf_t[:, c]
                            last = nc.tensor.transpose(psX[:, b * P:(b + 1) * P], src, ident[:])
                    last.then_inc(xt_psum, 1)
                adjacency(2, 4)
                if do_post:
                    if isinstance(t, int) and t == 2 and n == 0:
                        pe.wait_ge(step_u_in, 32)
                    pe.wait_ge(xt_ready, g4 + 1)
                    for s, u in ((0, u1), (1, u2)):
                        for k in range(KT):
                            last = nc.tensor.matmul(psZ, xT[:, s * KT + k, :], u[:, k, :],
                                                    start=(s + k == 0), stop=(s + k == KT))
                    last.then_inc(z_psum, 1)
                    if n == 0:
                        for w in range(2):
                            for k in range(KT):
                                last = nc.tensor.matmul(psX[:, w * P:(w + 1) * P], wkq[:, w, k, :], xT[:, KT + k, :],
                                                        start=(k == 0), stop=(k == KT - 1))
                        last.then_inc(kq_psum, 1)
                adjacency(4, 5)
                if has(t, 1):
                    transposes(0)
                    adjacency(5, 6)
                    transposes(1)
                    attention(0)
                    transposes(2)
                    adjacency(6, 8)
                    attention(1)
                    transposes(3)
                if has(t, -2):
                    pe.wait_ge(q_in[par], 16 * (n * NT // 2 + half + 2 - par))
                    logits(t + 2, par, 0)
                    logits(t + 2, par, 1)
                if has(t, 1):
                    attention(2)
                if has(t, 1):
                    attention(3)
                if has(t, -2):
                    logits(t + 2, par, 2)
                if has(t, -2):
                    logits(t + 2, par, 3)

            sweep(pe, body)

        @block.scalar
        def _(act):
            def normed(i):
                if i % PT == 0:
                    act.wait_ge(norm_ready, i // PT + 1)
                nc.scalar.activation(XA[:, i, 0:D], XF[:, i, 0:D], ACT.Relu, bias=nmr[:, i:i + 1],
                                     scale=rstd[:, i:i + 1]).then_inc(h_ready, 1)

            for i in range(3 * GR):
                normed(i)
            for g in range(NG):
                act.wait_ge(first_kq_psum, g + 1)
                nc.scalar.copy(KH[:, group(g)], first_k_ps[g % 2])
                nc.scalar.copy(M[0][:, group(g)].bitcast(F32R), first_q_ps[g % 2]).then_inc(first_hi, 1)
                for i in range((g + 3) * GR, min((g + 4) * GR, NT)):
                    normed(i)

            def body(n, t, par, half):
                G = n * NT + t

                def relu_sum(p, g, k):
                    act.drain()
                    act.wait_ge(guess_ready, EVALS * g + k + 1)
                    nc.scalar.activation(sink[:], E[p][:], ACT.Relu, bias=nthr[p], accum_out=rsum[p])

                def sign_sum(p):
                    act.drain()
                    nc.scalar.activation(sink[:], E[p][:], ACT.Sign, bias=nthr[p], accum_out=ssum[p]).then_inc(sums_ready, 1)

                def powers(p, g, k):
                    act.wait_ge(fracs_ready, EVALS * g + k + 1)
                    nc.scalar.activation(power[p], bits[p], ACT.Exp, bias=pbias,
                                         scale=QP * math.log(2) / 2 ** 23).then_inc(powers_ready, 1)

                def evacuate(q):
                    if has(t, 1):
                        act.wait_ge(block_ready, 4 * (G - 1) + q + 1)
                        nc.scalar.copy(AT[:, q * 1024:(q + 1) * 1024], psT_all).then_inc(at_ready, 1)

                if has(t, 0):
                    relu_sum(par, G, 2)
                    sign_sum(par)
                if has(t, 2):
                    act.wait_ge(scales_ready, G - 1)
                    last = nc.scalar.activation(xf_t[:], psR[:, 0:D], ACT.Copy, scale=rs)
                    if n == 0:
                        last = nc.scalar.activation(XF[:, t - 2, 0:D], psR[:, 0:D], ACT.Copy, scale=rs)
                    last.then_inc(adj_taken, 1)
                    act.wait_ge(attn_done, G - 1)
                    if n == 0 and not (isinstance(t, int) and t == 2):
                        act.wait_ge(xa_stored, 16 * (t - 2))
                    nc.scalar.activation(xa_t[:], psA[:, 0:D], ACT.Copy, scale=al1).then_inc(mixed_ready, 1)
                if has(t, 0):
                    powers(par, G, 2)
                p = (par + 1) % 2
                s1 = has(t, -1)
                if s1:
                    act.wait_ge(rowmax_ready, G + 2)
                    nc.scalar.activation(E[p][:], E[p][:], ACT.Exp, bias=negmax[p], scale=-1.0,
                                         accum_out=total[p]).then_inc(exp_ready, 1)
                if has(t, 2):
                    act.wait_ge(xt_psum, G - 1)
                    nc.scalar.copy(xT[:, :, :].rearrange("p k n -> p (k n)"), psX).then_inc(xt_ready, 1)
                if s1:
                    relu_sum(p, G + 1, 0)
                    sign_sum(p)
                evacuate(0)
                if s1:
                    powers(p, G + 1, 0)
                evacuate(1)
                if s1:
                    relu_sum(p, G + 1, 1)
                evacuate(2)
                if s1:
                    sign_sum(p)
                    powers(p, G + 1, 1)
                evacuate(3)

            sweep(act, body)

        @block.vector
        def _(v):
            V = nc.vector

            def fence():
                v.drain()

            def rsqrt_guess(y, x):
                V.tensor_scalar(y.bitcast(I32), x.bitcast(I32), -0.5, float(0x5F3759DF), ALU.mult, ALU.add)

            def rsqrt(y, x, w):
                rsqrt_guess(y, x)
                for _ in range(NEWTON):
                    fence()
                    V.tensor_tensor(w, y, y, ALU.mult)
                    fence()
                    V.scalar_tensor_tensor(w, w, -0.5, x, ALU.mult, ALU.mult)
                    fence()
                    V.scalar_tensor_tensor(y, w, 1.5, y, ALU.add, ALU.mult)
                fence()

            V.memset(one, 1.0)
            V.memset(pbias, -127.0 * QP * math.log(2) - math.log(QS) + 0.5 * math.log(RELAX))
            V.memset(flag_a[:], 0.0)
            V.memset(XA[:, :, D:W], 1.0)
            row_stats = AT[:, 2 * KT * GR * P:2 * KT * GR * P + 6 * NT].rearrange("p (t s) -> p t s", s=6)

            def first_norm(i):
                ts = slice(i * PT, (i + 1) * PT)
                v.wait_ge(x_in[i], 16)
                V.memset(XF[:, ts, D:W], 1.0)
                for j in range(i * PT, (i + 1) * PT):
                    V.bn_stats(row_stats[:, j, :], XF[:, j, 0:D])
                fence()
                for j in range(i * PT, (i + 1) * PT):
                    V.bn_aggr(mv[:, j, :], row_stats[:, j, :])
                fence()
                V.tensor_scalar(nmr[:, ts], mv[:, ts, 1], LN_EPS, None, ALU.add)
                fence()
                rsqrt(rstd[:, ts], nmr[:, ts], tmpn[:, ts])
                V.scalar_tensor_tensor(nmr[:, ts], mv[:, ts, 0], -1.0, rstd[:, ts], ALU.mult, ALU.mult).then_inc(norm_ready, 1)

            def take_xt(g):
                v.wait_ge(first_xt_psum, g + 1)
                if g >= 2:
                    v.wait_ge(first_kq_psum, g - 1)
                a0 = g % 2 * KT * GR * P
                V.tensor_copy(AT[:, a0:a0 + KT * GR * P], first_xt_ps[g % 2]).then_inc(first_xt, 1)

            def low_parts(g):
                v.wait_ge(first_hi, g + 1)
                V.tensor_tensor(KL[:, group(g)], first_k_ps[g % 2], KH[:, group(g)].bitcast(F32), ALU.subtract)
                V.tensor_tensor(M[0][A:P, group(g)].bitcast(F32R), first_q_ps[g % 2][A:P, :], M[0][A:P, group(g)],
                                ALU.subtract).then_inc(first_lo, 1)

            first_norm(0)
            v.wait_ge(fold_psum, 1)
            V.tensor_copy(wkq[:, 1, :, :].rearrange("p k n -> p (k n)"), psA[:, 0:KT * P]).then_inc(fold_ready, 1)
            first_norm(1)
            take_xt(0)
            for g in range(NG):
                if g % 2 == 0 and g // 2 + 2 < PARTS:
                    first_norm(g // 2 + 2)
                if g + 1 < NG:
                    take_xt(g + 1)
                low_parts(g)

            def guess(p, n):
                a, b = GUESS[n]
                V.tensor_scalar(tt, total[p], b, None, ALU.add)
                fence()
                V.reciprocal(hh, tt)
                V.tensor_scalar(target[p], total[p], TOP_P, None, ALU.mult)
                fence()
                V.scalar_tensor_tensor(thr[p], total[p], a, hh, ALU.mult, ALU.mult)
                V.scalar_tensor_tensor(nthr[p], total[p], -a, hh, ALU.mult, ALU.mult).then_inc(guess_ready, 1)
                V.reciprocal(rtotal[p], total[p])
                fence()
                V.tensor_scalar(nrtotal[p], rtotal[p], -1.0, None, ALU.mult)

            def fractions(p, g, k, margin, flags=False):
                fence()
                if flags:
                    V.transpose(flag_b[:], flag_a[:])
                v.wait_ge(sums_ready, EVALS * g + k + 1)
                V.tensor_scalar(cnt, ssum[p], 0.5, N / 2 + margin, ALU.mult, ALU.add)
                V.tensor_scalar(frac[p][:, 0:1], ssum[p], 0.5 / N, 0.5, ALU.mult, ALU.add)
                V.tensor_scalar(frac[p][:, 2:3], ssum[p], -0.5 / N, 0.5, ALU.mult, ALU.add)
                fence()
                V.scalar_tensor_tensor(gm, cnt, thr[p], rsum[p], ALU.mult, ALU.add)
                if flags:
                    gather_blocks()
                fence()
                V.tensor_scalar(frac[p][:, 1:2], gm, rtotal[p], None, ALU.mult)
                V.tensor_scalar(frac[p][:, 3:4], gm, nrtotal[p], 1.0, ALU.mult, ALU.add)
                if flags:
                    gather_all()
                fence()
                V.tensor_scalar(bits[p], frac[p].bitcast(I32), float(107 << 23), None, ALU.max).then_inc(fracs_ready, 1)

            def advance(p):
                V.tensor_scalar(hh, dd, 0.5, 1.0, ALU.mult, ALU.add)
                fence()
                V.tensor_scalar(hh, hh, 0.5, 1.5, ALU.max, ALU.min)
                fence()
                V.scalar_tensor_tensor(thr[p], thr[p], hh, hh, ALU.mult, ALU.mult)
                fence()

            def update(p, g, k, last):
                v.wait_ge(powers_ready, EVALS * g + k + 1)
                V.tensor_tensor(dz, power[p][:, 0:2], power[p][:, 2:4], ALU.subtract)
                fence()
                V.tensor_tensor(spread[p], dz1, dz0, ALU.subtract)
                fence()
                V.scalar_tensor_tensor(dd, dz1, -quantile_of(TOP_P) * math.sqrt(RELAX), spread[p], ALU.add, ALU.mult)
                fence()
                V.tensor_scalar(hh, dd, 0.5, 1.0, ALU.mult, ALU.add)
                if last:
                    V.tensor_scalar(tt, cnt, FEW, 2.0, ALU.is_lt, ALU.mult)
                fence()
                V.tensor_scalar(hh, hh, 0.5, 2.5, ALU.max, ALU.min)
                fence()
                V.scalar_tensor_tensor(thr[p], thr[p], hh, hh, ALU.mult, ALU.mult)
                if last:
                    fence()
                    V.tensor_tensor(thr[p], thr[p], tt, ALU.add)
                else:
                    V.scalar_tensor_tensor(nthr[p], nthr[p], hh, hh, ALU.mult, ALU.mult).then_inc(guess_ready, 1)

            def list_below(p, half):
                c = slice(half * N // 2, (half + 1) * N // 2)
                V.scalar_tensor_tensor(M[p][:, c], E[p][:, c], thr[p], E[p][:, c], ALU.is_le, ALU.mult,
                                       accum_out=below2 if half else below)

            def segments(p, s0, s1):
                if s0 == 0:
                    fence()
                    V.scalar_tensor_tensor(order[:, 0:1], total[p], below, below2, ALU.subtract, ALU.subtract)
                for s in range(s0, s1):
                    w = N // SEGS
                    V.max(cand[:, 8 * s:8 * s + 8], M[p][:, s * w:(s + 1) * w])
                if s1 == SEGS:
                    fence()
                    V.tensor_reduce(top8, cand[:, 7::8], AX, ALU.max)

            def rounds(norm=False):
                for r in range(ROUNDS):
                    V.max(order[:, 1 + 8 * r:9 + 8 * r], cand[:])
                    if norm:
                        newton_step(2 * r)
                    fence()
                    if r < ROUNDS - 1:
                        V.match_replace(cand[:], order[:, 1 + 8 * r:9 + 8 * r], cand[:], -1.0)
                        if norm:
                            newton_step(2 * r + 1)
                        fence()

            def newton_step(i):
                y, x, w = rstd[:, 0:1], nmr[:, 0:1], tmpn[:, 0:1]
                if i % 3 == 0:
                    V.tensor_tensor(w, y, y, ALU.mult)
                elif i % 3 == 1:
                    V.scalar_tensor_tensor(w, w, -0.5, x, ALU.mult, ALU.mult)
                else:
                    V.scalar_tensor_tensor(y, w, 1.5, y, ALU.add, ALU.mult)

            def smallest_kept(p):
                V.tensor_tensor_scan(before[:], order[:], order[:], 0.0, ALU.add, ALU.max)
                V.tensor_tensor(bad, order[:, 0:1], target[p], ALU.is_ge)
                fence()
                V.scalar_tensor_tensor(spare[:], before[:, 0:DEPTH], target[p], order[:, 1:1 + DEPTH],
                                       ALU.is_ge, ALU.max)
                V.scalar_tensor_tensor(cand[:, 0:DEPTH], before[:, 0:DEPTH], target[p], order[:, 1:1 + DEPTH],
                                       ALU.is_ge, ALU.mult)
                V.scalar_tensor_tensor(bad, before[:, DEPTH - 1:DEPTH], target[p], bad, ALU.is_lt, ALU.add)
                fence()
                V.tensor_reduce(estar, spare[:], AX, ALU.min)
                V.tensor_reduce(anext, cand[:, 0:DEPTH], AX, ALU.max)
                fence()
                V.scalar_tensor_tensor(bad, estar, top8, bad, ALU.is_le, ALU.add)
                V.tensor_tensor(tie, anext, estar, ALU.is_ge)

            def window(p):
                list_below(p, 0)
                list_below(p, 1)
                segments(p, 0, SEGS)
                rounds()
                smallest_kept(p)

            def gather_flags():
                V.transpose(flag_b[:], flag_a[:])
                fence()
                gather_blocks()
                fence()
                gather_all()
                fence()

            def gather_blocks():
                for q in range(4):
                    V.tensor_reduce(anyf[0:1, q:q + 1], flag_b[32 * q:32 * q + 1, :], AX, ALU.max)

            def gather_all():
                V.tensor_reduce(anyi[0:1, 0:1], anyf[0:1, :], AX, ALU.max)

            def gathered():
                return V.value_load(anyi[0:1, 0:1], min_val=0, max_val=16)

            def anyof(flag):
                fence()
                V.tensor_copy(flag_a[:, 0:1], flag)
                fence()
                gather_flags()
                return gathered()

            def keep(p, e, half):
                c = slice(half * N // 2, (half + 1) * N // 2)
                V.scalar_tensor_tensor(M[p][:, c], E[p][:, c], e, E[p][:, c], ALU.is_ge, ALU.mult,
                                       accum_out=kept[half][p])

            def refine(p):
                V.scalar_tensor_tensor(gm, thr[p], MARGIN, order[:, 0:1], ALU.mult, ALU.add)
                fence()
                V.tensor_scalar(gm, gm, rtotal[p], -TOP_P, ALU.mult, ALU.add)
                fence()
                V.scalar_tensor_tensor(dd, gm, 1.0 / (DENSITY * math.sqrt(RELAX)), spread[p], ALU.mult, ALU.mult)
                fence()
                advance(p)
                window(p)
                fence()
                V.scalar_tensor_tensor(take, bad, 0.0, openr, ALU.is_equal, ALU.mult)
                fence()
                V.copy_predicated(res, take.bitcast(I32), estar)
                V.copy_predicated(restie, take.bitcast(I32), tie)
                V.tensor_tensor(openr, openr, take, ALU.subtract)

            def by_bits(p):
                V.memset(lo_bits[:], 0)
                V.memset(one_bit[:], 1 << 29)
                with v.Fori(0, 30) as _:
                    fence()
                    V.tensor_tensor(try_bits[:], lo_bits[:], one_bit[:], ALU.bitwise_or)
                    fence()
                    V.tensor_scalar(one_bit[:], one_bit[:], 1, None, ALU.logical_shift_right)
                    V.scalar_tensor_tensor(M[p][:], E[p][:], try_bits[:].bitcast(F32), E[p][:], ALU.is_ge, ALU.mult,
                                           accum_out=gab)
                    fence()
                    V.tensor_tensor(take, gab, target[p], ALU.is_ge)
                    fence()
                    V.copy_predicated(lo_bits[:], take.bitcast(I32), try_bits[:])
                fence()
                V.copy_predicated(res, openr.bitcast(I32), lo_bits[:].bitcast(F32))
                V.copy_predicated(restie, openr.bitcast(I32), one)

            def drop_ties(p):
                V.tensor_scalar(E[p][:], M[p][:], res, None, ALU.is_equal)
                V.tensor_scalar(ylim, res, 1e-37, None, ALU.max)
                V.tensor_tensor(gab, kept[0][p], kept[1][p], ALU.add)
                fence()
                V.tensor_tensor_scan(E[p][:], E[p][:], E[p][:], 0.0, ALU.add, ALU.max)
                V.reciprocal(ylim, ylim)
                V.tensor_tensor(gab, target[p], gab, ALU.subtract)
                fence()
                V.scalar_tensor_tensor(gab, E[p][:, N - 1:N], res, gab, ALU.mult, ALU.add)
                fence()
                V.tensor_tensor(ylim, ylim, gab, ALU.mult)
                fence()
                V.tensor_scalar(ylim, ylim, 1.0, None, ALU.add)
                fence()
                V.scalar_tensor_tensor(E[p][:], E[p][:], ylim, M[p][:], ALU.is_ge, ALU.mult)
                fence()
                V.scalar_tensor_tensor(M[p][:], E[p][:], res, M[p][:], ALU.not_equal, ALU.mult, accum_out=kept[0][p])
                V.memset(kept[1][p], 0.0)

            def slow(p):
                V.tensor_scalar(openr, bad, 0.0, None, ALU.is_gt)
                V.tensor_copy(res, estar)
                V.tensor_copy(restie, tie)
                refine(p)
                with v.If(anyof(openr) > 0):
                    with v.Fori(0, REFINES - 1) as _:
                        with v.If(anyof(openr) > 0):
                            refine(p)
                        with v.Else():
                            v.nop()
                        v.nop()
                    with v.If(anyof(openr) > 0):
                        by_bits(p)
                    with v.Else():
                        v.nop()
                    v.nop()
                with v.Else():
                    v.nop()
                fence()
                keep(p, res, 0)
                keep(p, res, 1)
                with v.If(anyof(restie) > 0):
                    drop_ties(p)
                with v.Else():
                    v.nop()
                v.nop()

            def body(n, t, par, half):
                G = n * NT + t
                X_adj = XA if n == 0 else XF
                p0, p1 = par, (par + 1) % 2
                s1, s2, s4 = has(t, -1), has(t, 0), has(t, 2)
                g4 = G - 2

                def take_logits(c):
                    v.wait_ge(logits_ready, NLC * (G + 1) + c + 1)
                    V.tensor_scalar(E[p1][:, c * LC:(c + 1) * LC], psL[:, c % 2, :], -1.0, None, ALU.mult, ALU.min,
                                    accum_out=cmin[p1][:, c:c + 1]).then_inc(logits_taken, 1)

                if s1:
                    take_logits(0)
                if s4:
                    v.wait_ge(adj_used, NPC * (G - 1))
                    V.reciprocal(rs, psR[:, D:W]).then_inc(scales_ready, 1)
                if s1:
                    for c in range(1, NLC):
                        take_logits(c)
                    fence()
                    V.tensor_reduce(negmax[p1], cmin[p1], AX, ALU.min).then_inc(rowmax_ready, 1)
                if s2:
                    fractions(p0, G, 2, MARGIN)
                if s2:
                    update(p0, G, 2, True)
                if s2:
                    fence()
                    if not (n == 0 and isinstance(t, int) and t < 2):
                        v.wait_ge(block_ready, 4 * (G - 1))
                    elif t == 0:
                        v.wait_ge(q_stored, 16 * NG)
                    list_below(p0, 0)
                if s1:
                    v.wait_ge(exp_ready, G + 2)
                    guess(p1, n)
                if s2:
                    list_below(p0, 1)
                if s4:
                    v.wait_ge(z_psum, g4 + 1)
                    if n == 0:
                        if not (isinstance(t, int) and t == 2):
                            v.wait_ge(z_stored, 16 * (t - 2))
                        V.tensor_tensor(z_t[:], psZ, XA[:, t - 2, 0:D], ALU.add).then_inc(z_ready, 1)
                    else:
                        v.wait_ge(tail_in, 32 * (t - 1))
                        V.tensor_tensor(z_t[:], psZ, z_t[:], ALU.add).then_inc(z_ready, 1)
                if s4 and n == 0:
                    v.wait_ge(kq_psum, g4 + 1)
                    if not (isinstance(t, int) and t == 2):
                        v.wait_ge(kq_stored, 48 * (t - 2))
                    V.tensor_copy(hi_t[:, :, :].rearrange("p a n -> p (a n)"), psX[:, 0:2 * P])
                    fence()
                    V.tensor_tensor(kl_t[:], psX[:, 0:P], hi_t[:, 0, :].bitcast(F32), ALU.subtract)
                    V.tensor_tensor(hi_t[A:P, 1, :], psX[A:P, P:2 * P], hi_t[A:P, 1, :].bitcast(F32),
                                    ALU.subtract).then_inc(kq_ready, 1)
                scale = has(t, 1)
                norm = s4 and n == 1
                if norm and isinstance(t, int) and t == 2:
                    v.wait_ge(step_u_in, 32 + 80)
                if s2:
                    segments(p0, 0, 12)
                elif norm:
                    fence()
                if scale:
                    V.scalar_tensor_tensor(al0, kept[0][p1], kept[1][p1], rtot4[p1], ALU.add, ALU.mult)
                if norm:
                    V.bn_stats(stats[:], z_t[:])
                if s1:
                    fractions(p1, G + 1, 0, 0.0)
                else:
                    fence()
                if scale:
                    V.tensor_scalar(al0, al0, 1e-12, None, ALU.max)
                if norm:
                    V.bn_aggr(mv[:, 0, :], stats[:])
                if s2:
                    segments(p0, 12, 14)
                if s1:
                    update(p1, G + 1, 0, False)
                else:
                    fence()
                if scale:
                    V.reciprocal(al1, al0)
                if norm:
                    V.tensor_scalar(nmr[:, 0:1], mv[:, 0, 1:2], LN_EPS, None, ALU.add)
                if s2:
                    segments(p0, 14, SEGS)
                else:
                    fence()
                if scale:
                    V.tensor_tensor(al1, al1, rtot4[p1], ALU.mult)
                if norm:
                    rsqrt_guess(rstd[:, 0:1], nmr[:, 0:1])
                    fence()
                if s2:
                    rounds(norm)
                elif norm:
                    for i in range(3 * NEWTON):
                        newton_step(i)
                        fence()
                if norm:
                    if not (isinstance(t, int) and t == 2):
                        v.wait_ge(out_stored, 16 * (t - 2))
                    V.tensor_scalar(y_t[:], z_t[:], mv[:, 0, 0:1], rstd[:, 0:1], ALU.subtract, ALU.mult).then_inc(y_normed, 1)
                if s2:
                    smallest_kept(p0)
                if s2:
                    keep(p0, estar, 0)
                fence()
                if s2:
                    V.scalar_tensor_tensor(flag_a[:, 0:1], bad, OPEN, tie, ALU.mult, ALU.add)
                if s1:
                    fractions(p1, G + 1, 1, 0.0, flags=s2)
                elif s2:
                    fence()
                    gather_flags()
                if s2:
                    flag = gathered()
                if s1:
                    update(p1, G + 1, 1, False)
                if s2:
                    keep(p0, estar, 1)
                    with v.If(flag > 0):
                        with v.If(flag > int(OPEN) - 1):
                            slow(p0)
                        with v.Else():
                            V.tensor_copy(res, estar)
                            V.tensor_copy(restie, tie)
                            fence()
                            drop_ties(p0)
                        v.nop()
                    with v.Else():
                        v.nop()
                    fence()
                    V.tensor_copy(rtot4[par], rtotal[par]).then_inc(masked_ready, 1)

            sweep(v, body)


def kernel(x, adj, L0_gnn_W1, L0_gnn_W2, L0_gnn_W3, L0_gnn_U1, L0_gnn_U2, L0_gnn_ln_g, L0_gnn_ln_b):
    import numpy as np
    import concourse.bacc as bacc
    from concourse.bass_utils import run_bass_kernel_spmd

    n, d = x.shape
    nt = n // P
    lay = np.ascontiguousarray
    arrays = {
        "x": lay(np.asarray(x).reshape(nt, P, d)),
        "adj": lay(np.asarray(adj).reshape(nt, P, nt, P).transpose(0, 3, 2, 1).reshape(nt, P, nt * P)),
        "w1": lay(np.asarray(L0_gnn_W1)),
        "w2t": lay(np.asarray(L0_gnn_W2).T),
        "w3t": lay(np.asarray(L0_gnn_W3).T),
        "u1t": lay(np.asarray(L0_gnn_U1).transpose(0, 2, 1)),
        "u2t": lay(np.asarray(L0_gnn_U2).transpose(0, 2, 1)),
        "ln_g": lay(np.broadcast_to(np.asarray(L0_gnn_ln_g), (P, d))),
        "ln_b": lay(np.broadcast_to(np.asarray(L0_gnn_ln_b), (P, d))),
    }
    nc = bacc.Bacc("TRN2", target_bir_lowering=False, num_devices=1)
    ins = [nc.dram_tensor(k + "_dram", a.shape, mybir.dt.from_np(a.dtype), kind="ExternalInput").ap() for k, a in arrays.items()]
    out = nc.dram_tensor("out", (nt, P, d), F32, kind="ExternalOutput").ap()
    adj_preln_kernel(nc, *ins, out)
    r = run_bass_kernel_spmd(nc, [{k + "_dram": a for k, a in arrays.items()}], core_ids=[0])
    return np.asarray(r.results[0]["out"]).reshape(n, d)
```
